# Optimizing a Trainium2 kernel written in Bass

```python
import numpy as np
import jax
import jax.numpy as jnp

def _softmax(x, axis=-1):
    return jax.nn.softmax(x, axis=axis)

def _gelu(x):
    return jax.nn.gelu(x, approximate=True)

def _silu(x):
    return jax.nn.silu(x)

def _sigmoid(x):
    return jax.nn.sigmoid(x)

def _layernorm(x, axis=-1, eps=1e-05):
    m = jnp.mean(x, axis=axis, keepdims=True)
    v = jnp.var(x, axis=axis, keepdims=True)
    return (x - m) / jnp.sqrt(v + eps)

def _scatter_add(tgt, idx, src, axis=0):
    return tgt.at[idx].add(src)

def _segment_sum(src, seg, n):
    return jax.ops.segment_sum(src, seg, n)
kernel_name = 'mk_sandwich_d1_jaxref_r8_a270ae'

def setup_inputs(seed: int=0):
    np.random.seed(seed)
    _w = jnp.asarray

    def _L0_attn_setup():
        import jax, jax.numpy as jnp
        import numpy as np
        DIM = 128
        CHUNK = 64
        STATE = 64
        DT_RANK = (DIM + 15) // 16
        EPS = 1e-06

        def _rmsnorm(x, w):
            var = jnp.mean(x * x, axis=-1, keepdims=True)
            return x * jax.lax.rsqrt(var + EPS) * w
        key = jax.random.key(seed)
        ks = jax.random.split(key, 6)
        B, L = (2, 512)
        x = jax.random.normal(ks[0], (B, L, DIM), dtype=jnp.float32)
        norm_w = jnp.ones((DIM,), dtype=jnp.float32)
        x_proj_w = jax.random.normal(ks[1], (DT_RANK + 2 * STATE, DIM), dtype=jnp.float32) * 0.02
        dt_proj_w = jax.random.normal(ks[2], (DIM, DT_RANK), dtype=jnp.float32) * 0.02
        dt_proj_b = jnp.zeros((DIM,), dtype=jnp.float32)
        A_log = jnp.zeros((DIM, STATE), dtype=jnp.float32)
        D = jnp.ones((DIM,), dtype=jnp.float32)
        out_proj_w = jax.random.normal(ks[3], (DIM, DIM), dtype=jnp.float32) * 0.02
        return {'x': x, 'norm_w': norm_w, 'x_proj_w': x_proj_w, 'dt_proj_w': dt_proj_w, 'dt_proj_b': dt_proj_b, 'A_log': A_log, 'D': D, 'out_proj_w': out_proj_w}
    _L0_attn_in = _L0_attn_setup()

    def _L0_ffn_setup():
        import jax, jax.numpy as jnp
        import numpy as np
        D_MODEL = 128
        N_EXPERTS = 8
        TOP_K = 2
        FFN_HIDDEN = 4 * D_MODEL
        key = jax.random.key(seed)
        ks = jax.random.split(key, 6)

        def xavier(k, shape):
            fan_in, fan_out = (shape[-2], shape[-1])
            lim = jnp.sqrt(6.0 / (fan_in + fan_out))
            return jax.random.uniform(k, shape, jnp.float32, -lim, lim)
        x = jax.random.normal(ks[0], (4, 256, D_MODEL), jnp.float32)
        w_gate = xavier(ks[1], (N_EXPERTS, D_MODEL))
        W1 = xavier(ks[2], (N_EXPERTS, D_MODEL, FFN_HIDDEN))
        b1 = jnp.zeros((N_EXPERTS, FFN_HIDDEN), jnp.float32)
        W2 = xavier(ks[3], (N_EXPERTS, FFN_HIDDEN, D_MODEL))
        b2 = jnp.zeros((N_EXPERTS, D_MODEL), jnp.float32)
        return {'x': x, 'w_gate': w_gate, 'W1': W1, 'b1': b1, 'W2': W2, 'b2': b2}
    _L0_ffn_in = _L0_ffn_setup()
    _d = {'L0_attn_x': _L0_attn_in['x'], 'L0_attn_norm_w': _L0_attn_in['norm_w'], 'L0_attn_x_proj_w': _L0_attn_in['x_proj_w'], 'L0_attn_dt_proj_w': _L0_attn_in['dt_proj_w'], 'L0_attn_dt_proj_b': _L0_attn_in['dt_proj_b'], 'L0_attn_A_log': _L0_attn_in['A_log'], 'L0_attn_D': _L0_attn_in['D'], 'L0_attn_out_proj_w': _L0_attn_in['out_proj_w'], 'L0_ffn_w_gate': _L0_ffn_in['w_gate'], 'L0_ffn_W1': _L0_ffn_in['W1'], 'L0_ffn_b1': _L0_ffn_in['b1'], 'L0_ffn_W2': _L0_ffn_in['W2'], 'L0_ffn_b2': _L0_ffn_in['b2']}
    _x0 = _d['L0_attn_x']
    _d['L0_attn_x'] = jax.random.normal(jax.random.fold_in(jax.random.key(seed), 1), (8, 512, 128), dtype=_x0.dtype)
    del _x0
    return _d

def reference(L0_attn_x, L0_attn_norm_w, L0_attn_x_proj_w, L0_attn_dt_proj_w, L0_attn_dt_proj_b, L0_attn_A_log, L0_attn_D, L0_attn_out_proj_w, L0_ffn_w_gate, L0_ffn_W1, L0_ffn_b1, L0_ffn_W2, L0_ffn_b2):

    def _L0_attn_ref(x, norm_w, x_proj_w, dt_proj_w, dt_proj_b, A_log, D, out_proj_w):
        import jax, jax.numpy as jnp
        import numpy as np
        DIM = 128
        CHUNK = 64
        STATE = 64
        DT_RANK = (DIM + 15) // 16
        EPS = 1e-06

        def _rmsnorm(x, w):
            var = jnp.mean(x * x, axis=-1, keepdims=True)
            return x * jax.lax.rsqrt(var + EPS) * w
        B, L, Dm = x.shape
        assert L % CHUNK == 0
        nc = L // CHUNK
        M = B * nc
        xn = _rmsnorm(x, norm_w)
        proj = jnp.einsum('bld,pd->blp', xn, x_proj_w)
        delta_lo, Bs, Cs = jnp.split(proj, [DT_RANK, DT_RANK + STATE], axis=-1)
        delta = jax.nn.softplus(jnp.einsum('blr,dr->bld', delta_lo, dt_proj_w) + dt_proj_b)
        A = -jnp.exp(A_log)

        def to_tm(t, feat):
            return t.reshape(B, nc, CHUNK, feat).reshape(M, CHUNK, feat).transpose(1, 0, 2)
        dt_seq = to_tm(delta, Dm)
        b_seq = to_tm(Bs, STATE)
        c_seq = to_tm(Cs, STATE)
        x_seq = to_tm(xn, Dm)

        def step(h, inp):
            dt, bt, ct, xt = inp
            dA = jnp.exp(dt[..., None] * A)
            h = dA * h + dt[..., None] * bt[:, None, :] * xt[..., None]
            y = jnp.einsum('mdn,mn->md', h, ct)
            return (h, y)
        h0 = jnp.zeros((M, Dm, STATE), dtype=x.dtype)
        _, ys = jax.lax.scan(step, h0, (dt_seq, b_seq, c_seq, x_seq))
        y = ys.transpose(1, 0, 2).reshape(B, nc, CHUNK, Dm).reshape(B, L, Dm)
        return jnp.einsum('bld,od->blo', y + x * D, out_proj_w)

    def _L0_ffn_ref(x, w_gate, W1, b1, W2, b2):
        import jax, jax.numpy as jnp
        import numpy as np
        D_MODEL = 128
        N_EXPERTS = 8
        TOP_K = 2
        FFN_HIDDEN = 4 * D_MODEL
        B, S, D = x.shape
        flat_x = x.reshape(-1, D)
        gate = jax.nn.softmax(flat_x @ w_gate.T, axis=-1)
        topk_scores, topk_idx = jax.lax.top_k(gate, TOP_K)
        cw = (jax.nn.one_hot(topk_idx, N_EXPERTS, dtype=flat_x.dtype) * topk_scores[..., None]).sum(axis=1)
        h = jax.nn.gelu(jnp.einsum('td,edh->teh', flat_x, W1) + b1, approximate=False)
        y = jnp.einsum('teh,ehd->ted', h, W2) + b2
        out = jnp.einsum('ted,te->td', y, cw)
        return out.reshape(B, S, D)
    x = L0_attn_x
    x = x + _layernorm(_L0_attn_ref(_layernorm(x, axis=-1), L0_attn_norm_w, L0_attn_x_proj_w, L0_attn_dt_proj_w, L0_attn_dt_proj_b, L0_attn_A_log, L0_attn_D, L0_attn_out_proj_w), axis=-1)
    x = x + _layernorm(_L0_ffn_ref(_layernorm(x, axis=-1), L0_ffn_w_gate, L0_ffn_W1, L0_ffn_b1, L0_ffn_W2, L0_ffn_b2), axis=-1)
    return x

_drawn_inputs = setup_inputs


def setup_inputs(seed=0):
    import zlib

    import numpy as np

    out = dict(_drawn_inputs(seed))
    spreads = {'L0_attn_norm_w': (1.0, 0.2),
     'L0_attn_dt_proj_b': (0.0, 0.1),
     'L0_attn_A_log': (0.0, 0.1),
     'L0_attn_D': (1.0, 0.2),
     'L0_ffn_b1': (0.0, 0.1),
     'L0_ffn_b2': (0.0, 0.1)}
    factors = {'L0_attn_dt_proj_w': 2.715}
    for name, (base, spread) in spreads.items():
        noise = np.random.default_rng([zlib.crc32(name.encode()), seed]).standard_normal(out[name].shape)
        drawn = base * np.exp(spread * noise) if base else spread * noise
        out[name] = jnp.asarray(drawn.astype(out[name].dtype))
    for name, factor in factors.items():
        out[name] = (out[name] * factor).astype(out[name].dtype)
    return out
```

```python
from contextlib import ExitStack

import concourse.bass as bass
from concourse import mybir

ALU = mybir.AluOpType
ACT = mybir.ActivationFunctionType
AXIS_X = mybir.AxisListType.X
F32 = mybir.dt.float32
BF16 = mybir.dt.bfloat16

P = 128
DIM = 128
STATE = 64
CHUNK = 64
TOK = 512
TILES = TOK // P
CHUNKS = TOK // CHUNK
DT_RANK = 8
EXPERTS = 8
HID = 512
KT = HID // P
GROUP = 32
GROUPS = 2 * STATE // GROUP
PARTS = 3
DECAY_RING = 8
GELU_RING = 4
LN_EPS = 1e-5
RMS_EPS = 1e-6
EXPERT_AT = [8 + 7 * e for e in range(EXPERTS)]


def wait_for(eng, sem, count):
    if isinstance(count, int) and count <= 0:
        return
    eng.wait_ge(sem, count)


def sandwich_kernel(nc, x, norm_w, x_proj_wT, dt_proj_wT, dt_proj_b, A_log, D, out_proj_wT,
                    w_gateT, W1, b1, W2, b2, ident_in, earlier_in, out):
    B = x.shape[0]
    x_dram = x.rearrange("b (j p) d -> b p j d", p=P)
    out_dram = out.rearrange("b (j p) d -> b p j d", p=P)

    with ExitStack() as ctx:
        def sb(name, shape, dt=F32):
            return ctx.enter_context(nc.sbuf_tensor(name, shape, dt))

        def bank(name):
            return ctx.enter_context(nc.psum_tensor(name, [P, TOK], F32))

        def sem(name):
            return ctx.enter_context(nc.semaphore(name))

        ident = sb("ident", [P, P])
        ident3 = sb("ident3", [PARTS * GROUP, GROUP])
        select = sb("select", [PARTS * GROUP, GROUP, P], BF16)
        earlier = sb("earlier", [P, EXPERTS, EXPERTS])
        minus_half = sb("minus_half", [P, TILES])
        w_norm = sb("w_norm", [P, 1])
        w_xproj = sb("w_xproj", [P, DT_RANK + 2 * STATE])
        w_dt = sb("w_dt", [DT_RANK, DIM])
        b_dt = sb("b_dt", [P, 1])
        a_log = sb("a_log", [P, STATE])
        a_exp = sb("a_exp", [P, STATE])
        a_neg = sb("a_neg", [P, STATE])
        d_skip = sb("d_skip", [P, 1])
        w_out = sb("w_out", [P, DIM])
        w_gate = sb("w_gate", [P, EXPERTS])
        w_up = sb("w_up", [P, EXPERTS, HID])
        b_up = sb("b_up", [P, EXPERTS, KT])
        w_down = sb("w_down", [P, EXPERTS, KT, DIM])
        b_down = sb("b_down", [EXPERTS, DIM])

        x_in = [sb(f"x_in{i}", [P, TILES, DIM]) for i in range(2)]
        stats = sb("stats", [P, TILES, 6])
        mean_sum = sb("mean_sum", [P, TILES])
        mean_gap = sb("mean_gap", [P, TILES])
        squares = sb("squares", [P, TILES])
        mean = sb("mean", [P, TILES])
        gap_part = sb("gap_part", [P, TILES])
        within = sb("within", [P, TILES])
        var = sb("var", [P, TILES])
        rms_eps = sb("rms_eps", [P, TILES])
        var_eps = sb("var_eps", [P, TILES])
        rstd = sb("rstd", [P, TILES])
        rms_t = sb("rms_t", [P, TILES])
        rms_v = sb("rms_v", [P, TILES])
        rms_e = sb("rms_e", [P, TILES])
        rms = sb("rms", [P, TILES])
        rstd_rms = sb("rstd_rms", [P, TILES])
        z_tok = sb("z_tok", [P, TILES, DIM])
        zn_tok = sb("zn_tok", [P, TILES, DIM])
        attn_ln = sb("attn_ln", [P, TILES, DIM])
        x_mid = sb("x_mid", [P, TILES, DIM])
        z2_tok = sb("z2_tok", [P, TILES, DIM])
        gate_max = sb("gate_max", [P, TILES])
        gate_l = sb("gate_l", [P, TILES, EXPERTS])
        gate_e = sb("gate_e", [P, TILES, EXPERTS])
        gate_s = sb("gate_s", [P, TILES])
        gate_r = sb("gate_r", [P, TILES])
        gate_p = sb("gate_p", [P, TILES, EXPERTS])
        above = sb("above", [P, TILES, EXPERTS, EXPERTS])
        tied = sb("tied", [P, TILES, EXPERTS, EXPERTS])
        tied_earlier = sb("tied_earlier", [P, TILES, EXPERTS, EXPERTS])
        ahead = sb("ahead", [P, TILES, EXPERTS, EXPERTS])
        rank = sb("rank", [P, TILES, EXPERTS])
        combine = sb("combine", [P, TILES, EXPERTS])
        ffn_acc = sb("ffn_acc", [P, TILES, DIM])
        ffn_ln = sb("ffn_ln", [P, TILES, DIM])
        out_tile = sb("out_tile", [P, TILES, DIM])

        xnT = sb("xnT", [P, TOK])
        low = sb("low", [DT_RANK, TOK])
        bc_hi = sb("bc_hi", [P, TOK], BF16)
        bc_rest = sb("bc_rest", [P, TOK])
        bc_mid = sb("bc_mid", [P, TOK], BF16)
        bc_lo = sb("bc_lo", [P, TOK], BF16)
        bc_parts = [[sb(f"bc_parts{i}_{g}", [PARTS * GROUP, TOK], BF16) for g in range(GROUPS)] for i in range(2)]
        soft_pos = sb("soft_pos", [P, TOK])
        soft_abs = sb("soft_abs", [P, TOK])
        soft_exp = sb("soft_exp", [P, TOK])
        soft_log = sb("soft_log", [P, TOK])
        delta = [sb(f"delta{i}", [P, TOK]) for i in range(2)]
        delta_x = [sb(f"delta_x{i}", [P, TOK]) for i in range(2)]
        decay = [sb(f"decay{i}", [P, TOK]) for i in range(DECAY_RING)]
        drive = [sb(f"drive{i}", [P, TOK]) for i in range(2)]
        state = [sb(f"state{i}", [P, TOK]) for i in range(2)]
        term = [sb(f"term{i}", [P, TOK]) for i in range(4)]
        y_acc = [sb(f"y_acc{i}", [P, TOK]) for i in range(2)]
        z2T = sb("z2T", [P, TOK])
        combineT = sb("combineT", [EXPERTS, TOK])
        hidden = [sb(f"hidden{i}", [P, TOK]) for i in range(GELU_RING)]

        b_rows = [bank(f"b_rows{i}") for i in range(2)]
        c_rows = [bank(f"c_rows{i}") for i in range(2)]
        h_bank = [bank(f"h_bank{i}") for i in range(2)]
        y_bank = bank("y_bank")
        misc = bank("misc")
        misc_tok = misc[:, :].rearrange("p (j d) -> p j d", j=TILES)
        misc_gate = misc[:, 0:TILES * EXPERTS].rearrange("p (j e) -> p j e", j=TILES)
        y_tok = y_bank[:, :].rearrange("p (j d) -> p j d", j=TILES)

        weights_in = sem("weights_in")
        ffn_in = sem("ffn_in")
        decay_zeroed = sem("decay_zeroed")
        half_set = sem("half_set")
        select_built = sem("select_built")
        a_exp_done = sem("a_exp_done")
        a_ready = sem("a_ready")
        x_loaded = [sem(f"x_loaded{i}") for i in range(2)]
        in_stats = sem("in_stats")
        in_halves = sem("in_halves")
        in_moments = sem("in_moments")
        in_var = sem("in_var")
        in_rstd = sem("in_rstd")
        in_rstd2 = sem("in_rstd2")
        in_rstd2v = sem("in_rstd2v")
        in_rms_e = sem("in_rms_e")
        in_rms = sem("in_rms")
        in_scales = sem("in_scales")
        z_ready = sem("z_ready")
        zn_turned = sem("zn_turned")
        xn_ready = sem("xn_ready")
        z_turned = sem("z_turned")
        skip_ready = sem("skip_ready")
        bc_ready = sem("bc_ready")
        hi_ready = sem("hi_ready")
        rest_ready = sem("rest_ready")
        mid_ready = sem("mid_ready")
        lo_ready = sem("lo_ready")
        parts_in = sem("parts_in")
        last_part_in = sem("last_part_in")
        low_ready = sem("low_ready")
        low_copied = sem("low_copied")
        dt_ready = sem("dt_ready")
        soft_split = sem("soft_split")
        abs_ready = sem("abs_ready")
        soft_exp_ready = sem("soft_exp_ready")
        soft_ready = sem("soft_ready")
        delta_ready = sem("delta_ready")
        drive_input_ready = sem("drive_input_ready")
        b_shown = sem("b_shown")
        c_shown = sem("c_shown")
        decay_ready = sem("decay_ready")
        drive_ready = sem("drive_ready")
        scanned = sem("scanned")
        term_ready = sem("term_ready")
        term_added = sem("term_added")
        attn_ready = sem("attn_ready")
        attn_stats = sem("attn_stats")
        attn_halves = sem("attn_halves")
        attn_moments = sem("attn_moments")
        attn_var = sem("attn_var")
        attn_rstd = sem("attn_rstd")
        attn_normed = sem("attn_normed")
        mid_sum = sem("mid_sum")
        mid_stats = sem("mid_stats")
        mid_halves = sem("mid_halves")
        mid_moments = sem("mid_moments")
        mid_var = sem("mid_var")
        mid_rstd = sem("mid_rstd")
        z2_ready = sem("z2_ready")
        z2_turned = sem("z2_turned")
        z2T_ready = sem("z2T_ready")
        gate_shown = sem("gate_shown")
        gate_max_ready = sem("gate_max_ready")
        gate_l_ready = sem("gate_l_ready")
        gate_e_ready = sem("gate_e_ready")
        gate_s_ready = sem("gate_s_ready")
        gate_r_ready = sem("gate_r_ready")
        gate_p_ready = sem("gate_p_ready")
        compared = sem("compared")
        ties_ready = sem("ties_ready")
        ahead_ready = sem("ahead_ready")
        rank_ready = sem("rank_ready")
        combine_ready = sem("combine_ready")
        combine_turned = sem("combine_turned")
        combineT_ready = sem("combineT_ready")
        bias_shown = sem("bias_shown")
        ffn_acc_set = sem("ffn_acc_set")
        h_shown = sem("h_shown")
        hidden_ready = sem("hidden_ready")
        y_added = sem("y_added")
        expert_added = sem("expert_added")
        ffn_stats = sem("ffn_stats")
        ffn_halves = sem("ffn_halves")
        ffn_moments = sem("ffn_moments")
        ffn_var = sem("ffn_var")
        ffn_rstd = sem("ffn_rstd")
        ffn_normed = sem("ffn_normed")
        out_ready = sem("out_ready")
        out_stored = sem("out_stored")

        block = ctx.enter_context(nc.Block())

        def beats(eng, beat):
            beat(0, 0, 0, post=False)
            with eng.Fori(1, B // 2) as i:
                beat(2 * i - 1, i - 1, 1)
                beat(2 * i, i, 0)
            beat(B - 1, B // 2 - 1, 1, prep=False)
            beat(B, B // 2, 0, scan=False, prep=False)

        WEIGHTS = 13

        @block.sync
        def _(sp):
            sp.dma_start(x_in[0][:, :, :], x_dram[0]).then_inc(x_loaded[0], 16)
            sp.dma_start(ident[:, :], ident_in).then_inc(weights_in, 16)
            for s in range(PARTS):
                sp.dma_start(ident3[GROUP * s:GROUP * (s + 1), :], ident_in[0:GROUP, 0:GROUP]).then_inc(weights_in, 16)
            sp.dma_start(w_norm[:, :], norm_w.rearrange("(p a) -> p a", a=1)).then_inc(weights_in, 16)
            sp.dma_start(w_xproj[:, :], x_proj_wT).then_inc(weights_in, 16)
            sp.dma_start(w_dt[:, :], dt_proj_wT).then_inc(weights_in, 16)
            sp.dma_start(b_dt[:, :], dt_proj_b.rearrange("(p a) -> p a", a=1)).then_inc(weights_in, 16)
            sp.dma_start(a_log[:, :], A_log).then_inc(weights_in, 16)
            sp.dma_start(d_skip[:, :], D.rearrange("(p a) -> p a", a=1)).then_inc(weights_in, 16)
            sp.dma_start(w_out[:, :], out_proj_wT).then_inc(weights_in, 16)
            sp.dma_start(w_gate[:, :], w_gateT).then_inc(weights_in, 16)
            sp.dma_start(earlier[:, :, :], earlier_in).then_inc(weights_in, 16)
            sp.dma_start(x_in[1][:, :, :], x_dram[1]).then_inc(x_loaded[1], 16)

            def parts(g, par):
                sp.wait_ge(lo_ready, g + 1)
                for n in range(GROUPS):
                    for s, part in enumerate((bc_hi, bc_mid, bc_lo)):
                        if (n, s) != (GROUPS - 1, PARTS - 1):
                            sp.dma_start(bc_parts[par][n][GROUP * s:GROUP * (s + 1), :],
                                         part[GROUP * n:GROUP * (n + 1), :]).then_inc(parts_in, 16)

            def last_part(par):
                sp.dma_start(bc_parts[par][GROUPS - 1][GROUP * (PARTS - 1):GROUP * PARTS, :],
                             bc_lo[GROUP * (GROUPS - 1):GROUP * GROUPS, :]).then_inc(last_part_in, 16)

            parts(0, 0)
            last_part(0)
            sp.dma_start(w_up[:, :, :], W1.rearrange("e p h -> p e h")).then_inc(ffn_in, 16)
            sp.dma_start(b_up[:, :, :], b1).then_inc(ffn_in, 16)
            for e in range(EXPERTS):
                sp.dma_start(w_down[:, e, :, :], W2[e].rearrange("(k p) d -> p k d", p=P)).then_inc(ffn_in, 16)
            sp.dma_start(b_down[:, :], b2).then_inc(ffn_in, 16)

            def beat(b, half, par, post=True, scan=True, prep=True):
                if post and prep:
                    nxt = b + 1 if isinstance(b, int) else sp.snap(b + 1)
                    sp.wait_ge(mid_sum, b)
                    sp.dma_start(x_in[1 - par][:, :, :], x_dram[bass.ds(nxt, 1)].rearrange("a p j d -> (a p) j d")
                                 ).then_inc(x_loaded[1 - par], 16)
                if prep:
                    parts(b + 1, 1 - par)
                if post:
                    done = b - 1 if isinstance(b, int) else sp.snap(b - 1)
                    sp.wait_ge(out_ready, b)
                    sp.dma_start(out_dram[bass.ds(done, 1)].rearrange("a p j d -> (a p) j d"), out_tile[:, :, :]
                                 ).then_inc(out_stored, 16)
                    sp.wait_ge(out_stored, 16 * b)
                if prep:
                    last_part(1 - par)

            beats(sp, beat)

        FFN_LOADS = 3 + EXPERTS - 0

        @block.gpsimd
        def _(pool):
            nc.gpsimd.memset(rms_eps[:, :], RMS_EPS)
            nc.gpsimd.memset(minus_half[:, :], -0.5).then_inc(half_set, 1)
            pool.wait_ge(half_set, 1)

            def prep_rstd(g):
                pool.wait_ge(in_var, g + 1)
                nc.gpsimd.tensor_tensor(rstd[:, :], var_eps[:, :], minus_half[:, :], ALU.pow).then_inc(in_rstd, 1)
                pool.wait_ge(in_rstd, g + 1)
                nc.gpsimd.tensor_tensor(rms_t[:, :], rstd[:, :], rstd[:, :], ALU.mult).then_inc(in_rstd2, 1)
                pool.wait_ge(in_rstd2, g + 1)
                nc.gpsimd.tensor_tensor(rms_v[:, :], rms_t[:, :], var[:, :], ALU.mult).then_inc(in_rstd2v, 1)
                pool.wait_ge(in_rstd2v, g + 1)
                nc.gpsimd.tensor_tensor(rms_e[:, :], rms_v[:, :], rms_eps[:, :], ALU.add).then_inc(in_rms_e, 1)
                pool.wait_ge(in_rms_e, g + 1)
                nc.gpsimd.tensor_tensor(rms[:, :], rms_e[:, :], minus_half[:, :], ALU.pow).then_inc(in_rms, 1)
                pool.wait_ge(in_rms, g + 1)
                nc.gpsimd.tensor_tensor(rstd_rms[:, :], rms[:, :], rstd[:, :], ALU.mult).then_inc(in_scales, 1)

            prep_rstd(0)

            def beat(b, half, par, post=True, scan=True, prep=True):
                f = b - 1
                if scan:
                    pool.wait_ge(skip_ready, b + 1)
                for n in range(STATE if scan else 1):
                    if post and n == 3:
                        pass
                    if scan:
                        done = b * STATE + n
                        pool.wait_ge(term_ready, done + 1)
                        wait_for(pool, term_added, done)
                        nc.gpsimd.tensor_tensor(y_acc[par][:, :], y_acc[par][:, :], term[n % 4][:, :],
                                                ALU.add).then_inc(term_added, 1)
                    if post and n == (1 if scan else 0):
                        pool.wait_ge(attn_var, f + 1)
                        nc.gpsimd.tensor_tensor(rstd[:, :], var_eps[:, :], minus_half[:, :],
                                                ALU.pow).then_inc(attn_rstd, 1)
                    if post and n == (3 if scan else 0):
                        pool.wait_ge(mid_var, f + 1)
                        nc.gpsimd.tensor_tensor(rstd[:, :], var_eps[:, :], minus_half[:, :],
                                                ALU.pow).then_inc(mid_rstd, 1)
                    if prep and n == 16:
                        prep_rstd(b + 1)
                if post:
                    pool.wait_ge(ffn_var, f + 1)
                    nc.gpsimd.tensor_tensor(rstd[:, :], var_eps[:, :], minus_half[:, :],
                                            ALU.pow).then_inc(ffn_rstd, 1)

            beats(pool, beat)

        @block.scalar
        def _(act):
            act.wait_ge(weights_in, 16 * WEIGHTS)
            nc.scalar.activation(a_exp[:, :], a_log[:, :], ACT.Exp).then_inc(a_exp_done, 1)
            act.wait_ge(a_exp_done, 1)
            nc.scalar.mul(a_neg[:, :], a_exp[:, :], -1.0).then_inc(a_ready, 1)

            def prep(g, par, at):
                if at == 0:
                    act.wait_ge(zn_turned, g + 1)
                    wait_for(act, drive_input_ready, g)
                    nc.scalar.activation(xnT[:, :], misc[:, :], ACT.Copy, scale=w_norm[:, :]).then_inc(xn_ready, 1)
                if at == 1:
                    act.wait_ge(z_turned, g + 1)
                    wait_for(act, attn_ready, g - 1)
                    nc.scalar.activation(y_acc[par][:, :], misc[:, :], ACT.Copy, scale=d_skip[:, :]).then_inc(skip_ready, 1)
                if at == 2:
                    act.wait_ge(bc_ready, g + 1)
                    wait_for(act, parts_in, 16 * (PARTS * GROUPS - 1) * g)
                    wait_for(act, last_part_in, 16 * g)
                    nc.scalar.copy(bc_hi[:, :], misc[:, :]).then_inc(hi_ready, 1)
                if at == 3:
                    act.wait_ge(rest_ready, g + 1)
                    nc.scalar.copy(bc_mid[:, :], bc_rest[:, :]).then_inc(mid_ready, 1)
                if at == 4:
                    act.wait_ge(low_ready, g + 1)
                    nc.scalar.copy(low[:, :], misc[0:DT_RANK, :]).then_inc(low_copied, 1)
                if at == 5:
                    act.wait_ge(soft_split, g + 1)
                    nc.scalar.activation(soft_abs[:, :], misc[:, :], ACT.Abs, bias=b_dt[:, :]).then_inc(abs_ready, 1)
                    act.wait_ge(abs_ready, g + 1)
                    nc.scalar.activation(soft_exp[:, :], soft_abs[:, :], ACT.Exp, scale=-1.0).then_inc(soft_exp_ready, 1)
                    act.wait_ge(soft_exp_ready, g + 1)
                    nc.scalar.activation(soft_log[:, :], soft_exp[:, :], ACT.Ln, bias=1.0).then_inc(soft_ready, 1)

            for at in range(6):
                prep(0, 0, at)

            def beat(b, half, par, post=True, scan=True, prep_=True, prep_at=(20, 22, 28, 30, 35, 43)):
                f = b - 1

                def gelu(e, k):
                    unit = f * EXPERTS * KT + e * KT + k
                    act.wait_ge(h_shown, unit + 1)
                    if e > 0:
                        act.wait_ge(y_added, unit + 1 - GELU_RING)
                    nc.scalar.activation(hidden[k % GELU_RING][:, :], h_bank[k % 2][:, :], ACT.Gelu,
                                         bias=b_up[:, e, k:k + 1]).then_inc(hidden_ready, 1)

                if scan:
                    act.wait_ge(delta_ready, b + 1)
                if post:
                    act.wait_ge(ffn_in, 16 * FFN_LOADS)
                for step in range(STATE):
                    if scan:
                        n = step
                        done = b * STATE + n
                        if not (isinstance(b, int) and b == 0 and n < DECAY_RING):
                            act.wait_ge(scanned, done + 1 - DECAY_RING)
                        nc.scalar.activation(
                            decay[n % DECAY_RING][:, :].rearrange("p (c t) -> p c t", t=CHUNK)[:, :, 1:CHUNK],
                            delta[par][:, :].rearrange("p (c t) -> p c t", t=CHUNK)[:, :, 1:CHUNK],
                            ACT.Exp, scale=a_neg[:, n:n + 1]).then_inc(decay_ready, 1)
                    if post:
                        if step == 5:
                            act.wait_ge(z2_turned, f + 1)
                            nc.scalar.copy(z2T[:, :], misc[:, :]).then_inc(z2T_ready, 1)
                        if step == 8:
                            act.wait_ge(gate_l_ready, f + 1)
                            nc.scalar.activation(gate_e[:, :, :], gate_l[:, :, :], ACT.Exp).then_inc(gate_e_ready, 1)
                        for e in range(EXPERTS):
                            if step == min(EXPERT_AT[e] + 5, STATE - 1):
                                for k in range(KT):
                                    gelu(e, k)
                    if post and step == 14:
                        act.wait_ge(combine_turned, f + 1)
                        nc.scalar.copy(combineT[:, :], misc[0:EXPERTS, :]).then_inc(combineT_ready, 1)
                        act.wait_ge(bias_shown, f + 1)
                        nc.scalar.copy(ffn_acc[:, :, :], misc_tok).then_inc(ffn_acc_set, 1)
                    if prep_ and step in prep_at:
                        prep(b + 1, 1 - par, prep_at.index(step))

            beats(act, lambda b, half, par, post=True, scan=True, prep=True: beat(b, half, par, post, scan, prep))

        @block.tensor
        def _(pe):
            pe.wait_ge(weights_in, 16 * WEIGHTS)
            pe.wait_ge(select_built, 1)

            def prep(g, at, after_post):
                if at == 0:
                    pe.wait_ge(z_ready, g + 1)
                    wait_for(pe, soft_split, g)
                    wait_for(pe, abs_ready, g)
                    if after_post:
                        pe.wait_ge(ffn_acc_set, g - 1)
                    for j in range(TILES):
                        last = nc.tensor.transpose(misc[:, j * P:(j + 1) * P], zn_tok[:, j, :], ident[:, :])
                    last.then_inc(zn_turned, 1)
                if at == 1:
                    pe.wait_ge(xn_ready, g + 1)
                    for j in range(TILES):
                        last = nc.tensor.transpose(misc[:, j * P:(j + 1) * P], z_tok[:, j, :], ident[:, :])
                    last.then_inc(z_turned, 1)
                if at == 2:
                    pe.wait_ge(skip_ready, g + 1)
                    nc.tensor.matmul(misc[:, :], w_xproj[:, DT_RANK:], xnT[:, :], start=True, stop=True).then_inc(bc_ready, 1)
                if at == 3:
                    pe.wait_ge(hi_ready, g + 1)
                    pe.wait_ge(rest_ready, g + 1)
                    nc.tensor.matmul(misc[0:DT_RANK, :], w_xproj[:, 0:DT_RANK], xnT[:, :], start=True, stop=True).then_inc(low_ready, 1)
                if at == 4:
                    pe.wait_ge(low_copied, g + 1)
                    nc.tensor.matmul(misc[:, :], w_dt[:, :], low[:, :], start=True, stop=True).then_inc(dt_ready, 1)

            for at in range(5):
                prep(0, at, False)

            def beat(b, half, par, post=True, scan=True, prep_=True):
                f = b - 1

                def show_b(n):
                    wait_for(pe, drive_ready, b * STATE + n - 1)
                    nc.tensor.matmul(b_rows[n % 2][:, :], select[:, n % GROUP, :], bc_parts[par][n // GROUP][:, :],
                                     start=True, stop=True).then_inc(b_shown, 1)

                def show_c(n):
                    if n == GROUP:
                        pe.wait_ge(last_part_in, 16 * (b + 1))
                    wait_for(pe, term_ready, b * STATE + n - 1)
                    nc.tensor.matmul(c_rows[n % 2][:, :], select[:, n % GROUP, :],
                                     bc_parts[par][STATE // GROUP + n // GROUP][:, :],
                                     start=True, stop=True).then_inc(c_shown, 1)

                def states(n):
                    if scan and n < STATE:
                        if n + 1 < STATE:
                            show_b(n + 1)
                        show_c(n)

                def up(e, k):
                    unit = f * EXPERTS * KT + e * KT + k
                    if e > 0 or k >= 2:
                        pe.wait_ge(hidden_ready, unit - 1)
                    nc.tensor.matmul(h_bank[k % 2][:, :], w_up[:, e, k * P:(k + 1) * P], z2T[:, :],
                                     start=True, stop=True).then_inc(h_shown, 1)

                def down(e, k):
                    unit = f * EXPERTS * KT + e * KT + k
                    pe.wait_ge(hidden_ready, unit + 1)
                    if k == 0 and e > 0:
                        pe.wait_ge(expert_added, f * EXPERTS + e)
                    for j in range(TILES):
                        last = nc.tensor.matmul(y_tok[:, j, :], hidden[k % GELU_RING][:, j * P:(j + 1) * P],
                                                w_down[:, e, k, :], start=(k == 0 and j == 0), stop=(k == KT - 1),
                                                skip_group_check=True)
                    last.then_inc(y_added, 1)

                if scan:
                    pe.wait_ge(parts_in, 16 * (PARTS * GROUPS - 1) * (b + 1))
                    show_b(0)
                prep_at = (20, 21, 27, 34, 41)
                n = 0
                while n < STATE:
                    if post and n == 2:
                        pe.wait_ge(term_added, b * STATE)
                        pe.wait_ge(soft_split, b + (1 if scan else 0))
                        pe.wait_ge(abs_ready, b + (1 if scan else 0))
                        for j in range(TILES):
                            last = nc.tensor.matmul(misc_tok[:, j, :], y_acc[1 - par][:, j * P:(j + 1) * P],
                                                    w_out[:, :], start=True, stop=True)
                        last.then_inc(attn_ready, 1)
                    if post and n == 6:
                        pe.wait_ge(z2_ready, f + 1)
                        pe.wait_ge(attn_normed, f + 1)
                        for j in range(TILES):
                            last = nc.tensor.transpose(misc[:, j * P:(j + 1) * P], z2_tok[:, j, :], ident[:, :])
                        last.then_inc(z2_turned, 1)
                    if post and n == 7:
                        pe.wait_ge(z2T_ready, f + 1)
                        for j in range(TILES):
                            last = nc.tensor.matmul(misc_gate[:, j, :], z2T[:, j * P:(j + 1) * P], w_gate[:, :],
                                                    start=True, stop=True)
                        last.then_inc(gate_shown, 1)
                    if post and n == 13:
                        pe.wait_ge(combine_ready, f + 1)
                        pe.wait_ge(gate_l_ready, f + 1)
                        for j in range(TILES):
                            last = nc.tensor.transpose(misc[0:EXPERTS, j * P:(j + 1) * P], combine[:, j, :], ident[:, :])
                        last.then_inc(combine_turned, 1)
                        pe.wait_ge(combineT_ready, f + 1)
                        for j in range(TILES):
                            last = nc.tensor.matmul(misc_tok[:, j, :], combineT[:, j * P:(j + 1) * P], b_down[:, :],
                                                    start=True, stop=True)
                        last.then_inc(bias_shown, 1)
                    if prep_ and n in prep_at:
                        prep(b + 1, prep_at.index(n), post)
                    if post and n in EXPERT_AT:
                        e = EXPERT_AT.index(n)
                        if e == 0:
                            pe.wait_ge(ffn_in, 16 * FFN_LOADS)
                        up(e, 0)
                        up(e, 1)
                        states(n)
                        up(e, 2)
                        states(n + 1)
                        up(e, 3)
                        states(n + 2)
                        down(e, 0)
                        down(e, 1)
                        states(n + 3)
                        down(e, 2)
                        states(n + 4)
                        down(e, 3)
                        n += 5
                        continue
                    states(n)
                    n += 1

            beats(pe, lambda b, half, par, post=True, scan=True, prep=True: beat(b, half, par, post, scan, prep))

        @block.vector
        def _(dve):
            for i in range(DECAY_RING):
                last = nc.vector.memset(decay[i][:, :], 0.0)
            last.then_inc(decay_zeroed, 1)

            def token_stats(src, stats_sem, halves_sem, moments_sem, var_sem, count):
                for j in range(TILES):
                    last = nc.vector.bn_stats(stats[:, j, :], src[:, j, :])
                last.then_inc(stats_sem, 1)
                dve.wait_ge(stats_sem, count)
                nc.vector.tensor_tensor(mean_sum[:, :], stats[:, :, 1], stats[:, :, 4], ALU.add)
                nc.vector.tensor_tensor(mean_gap[:, :], stats[:, :, 1], stats[:, :, 4], ALU.subtract)
                nc.vector.tensor_tensor(squares[:, :], stats[:, :, 2], stats[:, :, 5], ALU.add).then_inc(halves_sem, 1)
                dve.wait_ge(halves_sem, count)
                nc.vector.tensor_scalar(mean[:, :], mean_sum[:, :], 0.5, None, ALU.mult)
                nc.vector.scalar_tensor_tensor(out=gap_part[:, :], in0=mean_gap[:, :], scalar=0.25, in1=mean_gap[:, :],
                                               op0=ALU.mult, op1=ALU.mult)
                nc.vector.tensor_scalar(within[:, :], squares[:, :], 1.0 / DIM, None, ALU.mult).then_inc(moments_sem, 1)
                dve.wait_ge(moments_sem, count)
                nc.vector.tensor_tensor(var[:, :], within[:, :], gap_part[:, :], ALU.add)
                nc.vector.scalar_tensor_tensor(out=var_eps[:, :], in0=within[:, :], scalar=LN_EPS, in1=gap_part[:, :],
                                               op0=ALU.add, op1=ALU.add).then_inc(var_sem, 1)

            def normalise(dst, src, scale):
                for j in range(TILES):
                    last = nc.vector.tensor_scalar(dst[:, j, :], src[:, j, :], mean[:, j:j + 1], scale[:, j:j + 1],
                                                   ALU.subtract, ALU.mult)
                return last

            def prep(g, half_g, par, at):
                if at == 0:
                    dve.wait_ge(x_loaded[par], 16 * (half_g + 1))
                    token_stats(x_in[par], in_stats, in_halves, in_moments, in_var, g + 1)
                if at == 1:
                    dve.wait_ge(in_scales, g + 1)
                    wait_for(dve, z_turned, g)
                    normalise(z_tok, x_in[par], rstd)
                    normalise(zn_tok, x_in[par], rstd_rms).then_inc(z_ready, 1)
                if at == 2:
                    dve.wait_ge(hi_ready, g + 1)
                    nc.vector.tensor_tensor(bc_rest[:, :], misc[:, :], bc_hi[:, :], ALU.subtract).then_inc(rest_ready, 1)
                if at == 3:
                    dve.wait_ge(mid_ready, g + 1)
                    nc.vector.tensor_tensor(bc_lo[:, :], bc_rest[:, :], bc_mid[:, :], ALU.subtract).then_inc(lo_ready, 1)
                if at == 4:
                    dve.wait_ge(dt_ready, g + 1)
                    nc.vector.tensor_scalar(soft_pos[:, :], misc[:, :], b_dt[:, :], 0.0, ALU.add,
                                            ALU.max).then_inc(soft_split, 1)
                if at == 5:
                    dve.wait_ge(soft_ready, g + 1)
                    wait_for(dve, decay_ready, (g - 1) * STATE)
                    nc.vector.tensor_tensor(delta[par][:, :], soft_log[:, :], soft_pos[:, :], ALU.add).then_inc(delta_ready, 1)
                    dve.wait_ge(delta_ready, g + 1)
                    nc.vector.tensor_tensor(delta_x[par][:, :], delta[par][:, :], xnT[:, :],
                                            ALU.mult).then_inc(drive_input_ready, 1)

            prep(0, 0, 0, 0)
            dve.wait_ge(weights_in, 16 * WEIGHTS)
            nc.vector.tensor_copy(select[:, :, :], ident3[:, :].rearrange("p (n a) -> p n a", a=1)
                                  .to_broadcast([PARTS * GROUP, GROUP, P])).then_inc(select_built, 1)
            for at in range(1, 6):
                prep(0, 0, 0, at)
            dve.wait_ge(a_ready, 1)

            def beat(b, half, par, post=True, scan=True, prep_=True):
                f = b - 1

                def drive_of(n):
                    done = b * STATE + n
                    dve.wait_ge(b_shown, done + 1)
                    nc.vector.tensor_tensor(drive[n % 2][:, :], delta_x[par][:, :], b_rows[n % 2][:, :],
                                            ALU.mult).then_inc(drive_ready, 1)

                def state_of(n):
                    done = b * STATE + n
                    dve.wait_ge(decay_ready, done + 1)
                    dve.wait_ge(drive_ready, done + 1)
                    nc.vector.tensor_tensor_scan(state[n % 2][:, :], decay[n % DECAY_RING][:, :], drive[n % 2][:, :],
                                                 0.0, ALU.mult, ALU.add).then_inc(scanned, 1)

                def term_of(n):
                    done = b * STATE + n
                    dve.wait_ge(c_shown, done + 1)
                    dve.wait_ge(scanned, done + 1)
                    wait_for(dve, term_added, done - 3)
                    nc.vector.tensor_tensor(term[n % 4][:, :], state[n % 2][:, :], c_rows[n % 2][:, :],
                                            ALU.mult).then_inc(term_ready, 1)

                def post_step(at):
                    if at == 0:
                        dve.wait_ge(attn_ready, f + 1)
                        token_stats(misc_tok, attn_stats, attn_halves, attn_moments, attn_var, f + 1)
                    if at == 1:
                        dve.wait_ge(attn_rstd, f + 1)
                        normalise(attn_ln, misc_tok, rstd).then_inc(attn_normed, 1)
                        dve.wait_ge(attn_normed, f + 1)
                        nc.vector.tensor_tensor(x_mid[:, :, :], attn_ln[:, :, :], x_in[1 - par][:, :, :],
                                                ALU.add).then_inc(mid_sum, 1)
                        dve.wait_ge(mid_sum, f + 1)
                        token_stats(x_mid, mid_stats, mid_halves, mid_moments, mid_var, f + 1)
                    if at == 2:
                        dve.wait_ge(mid_rstd, f + 1)
                        normalise(z2_tok, x_mid, rstd).then_inc(z2_ready, 1)
                    if at == 3:
                        dve.wait_ge(gate_shown, f + 1)
                        nc.vector.tensor_reduce(gate_max[:, :], misc_gate, AXIS_X, ALU.max).then_inc(gate_max_ready, 1)
                        dve.wait_ge(gate_max_ready, f + 1)
                        nc.vector.tensor_tensor(gate_l[:, :, :], misc_gate,
                                                gate_max[:, :].rearrange("p (j a) -> p j a", a=1)
                                                .to_broadcast([P, TILES, EXPERTS]), ALU.subtract).then_inc(gate_l_ready, 1)
                    if at == 4:
                        dve.wait_ge(gate_e_ready, f + 1)
                        nc.vector.tensor_reduce(gate_s[:, :], gate_e[:, :, :], AXIS_X, ALU.add).then_inc(gate_s_ready, 1)
                        dve.wait_ge(gate_s_ready, f + 1)
                        nc.vector.reciprocal(gate_r[:, :], gate_s[:, :]).then_inc(gate_r_ready, 1)
                        dve.wait_ge(gate_r_ready, f + 1)
                        nc.vector.tensor_tensor(gate_p[:, :, :], gate_e[:, :, :],
                                                gate_r[:, :].rearrange("p (j a) -> p j a", a=1)
                                                .to_broadcast([P, TILES, EXPERTS]), ALU.mult).then_inc(gate_p_ready, 1)
                        dve.wait_ge(gate_p_ready, f + 1)
                        for j in range(TILES):
                            this = gate_p[:, j, :].rearrange("p (e a) -> p e a", a=1).to_broadcast([P, EXPERTS, EXPERTS])
                            other = gate_p[:, j, :].rearrange("p (a e) -> p a e", a=1).to_broadcast([P, EXPERTS, EXPERTS])
                            nc.vector.tensor_tensor(above[:, j, :, :], other, this, ALU.is_gt)
                            last = nc.vector.tensor_tensor(tied[:, j, :, :], other, this, ALU.is_equal)
                        last.then_inc(compared, 1)
                        dve.wait_ge(compared, f + 1)
                        nc.vector.tensor_tensor(tied_earlier[:, :, :, :].rearrange("p j e o -> p j (e o)"),
                                                tied[:, :, :, :].rearrange("p j e o -> p j (e o)"),
                                                earlier[:, :, :].rearrange("p (a e) o -> p a (e o)", a=1)
                                                .to_broadcast([P, TILES, EXPERTS * EXPERTS]),
                                                ALU.mult).then_inc(ties_ready, 1)
                        dve.wait_ge(ties_ready, f + 1)
                        nc.vector.tensor_tensor(ahead[:, :, :, :], above[:, :, :, :], tied_earlier[:, :, :, :],
                                                ALU.add).then_inc(ahead_ready, 1)
                        dve.wait_ge(ahead_ready, f + 1)
                        nc.vector.tensor_reduce(rank[:, :, :], ahead[:, :, :, :], AXIS_X, ALU.add).then_inc(rank_ready, 1)
                        dve.wait_ge(rank_ready, f + 1)
                        nc.vector.scalar_tensor_tensor(out=combine[:, :, :], in0=rank[:, :, :], scalar=1.5,
                                                       in1=gate_p[:, :, :], op0=ALU.is_lt,
                                                       op1=ALU.mult).then_inc(combine_ready, 1)

                def add_expert(e):
                    dve.wait_ge(y_added, f * EXPERTS * KT + (e + 1) * KT)
                    dve.wait_ge(ffn_acc_set, f + 1)
                    if e > 0:
                        dve.wait_ge(expert_added, f * EXPERTS + e)
                    for j in range(TILES):
                        last = nc.vector.scalar_tensor_tensor(out=ffn_acc[:, j, :], in0=y_tok[:, j, :],
                                                              scalar=combine[:, j, e:e + 1], in1=ffn_acc[:, j, :],
                                                              op0=ALU.mult, op1=ALU.add)
                    last.then_inc(expert_added, 1)

                def finish():
                    dve.wait_ge(expert_added, (f + 1) * EXPERTS)
                    token_stats(ffn_acc, ffn_stats, ffn_halves, ffn_moments, ffn_var, f + 1)
                    dve.wait_ge(ffn_rstd, f + 1)
                    normalise(ffn_ln, ffn_acc, rstd).then_inc(ffn_normed, 1)
                    dve.wait_ge(ffn_normed, f + 1)
                    if not prep_:
                        dve.wait_ge(out_stored, 16 * f)
                    nc.vector.tensor_tensor(out_tile[:, :, :], ffn_ln[:, :, :], x_mid[:, :, :],
                                            ALU.add).then_inc(out_ready, 1)

                if scan:
                    dve.wait_ge(drive_input_ready, b + 1)
                    drive_of(0)
                post_at = (1, 3, 5, 7, 9)
                prep_at = (15, 19, 29, 32, 42, 46)
                for n in range(STATE):
                    if scan:
                        state_of(n)
                        if n + 1 < STATE:
                            drive_of(n + 1)
                        term_of(n)
                    if post and n in post_at:
                        post_step(post_at.index(n))
                    if prep_ and n in prep_at:
                        prep(b + 1, half + par, 1 - par, prep_at.index(n))
                    if post:
                        for e in range(EXPERTS):
                            if n == min(EXPERT_AT[e] + 7, STATE - 1):
                                add_expert(e)
                if post:
                    finish()

            beats(dve, lambda b, half, par, post=True, scan=True, prep=True: beat(b, half, par, post, scan, prep))


_INS = ['L0_attn_x', 'L0_attn_norm_w', 'x_proj_wT', 'dt_proj_wT', 'L0_attn_dt_proj_b', 'L0_attn_A_log', 'L0_attn_D',
        'out_proj_wT', 'w_gateT', 'L0_ffn_W1', 'b1_cols', 'L0_ffn_W2', 'L0_ffn_b2', 'ident', 'earlier']


def kernel(**inputs):
    import numpy as np
    import concourse.bacc as bacc
    from concourse.bass_utils import run_bass_kernel_spmd

    laid = {name: np.ascontiguousarray(a) for name, a in inputs.items()}
    laid['x_proj_wT'] = np.ascontiguousarray(laid['L0_attn_x_proj_w'].T)
    laid['dt_proj_wT'] = np.ascontiguousarray(laid['L0_attn_dt_proj_w'].T)
    laid['out_proj_wT'] = np.ascontiguousarray(laid['L0_attn_out_proj_w'].T)
    laid['w_gateT'] = np.ascontiguousarray(laid['L0_ffn_w_gate'].T)
    laid['b1_cols'] = np.ascontiguousarray(laid['L0_ffn_b1'].reshape(EXPERTS, KT, P).transpose(2, 0, 1))
    laid['ident'] = np.eye(P, dtype=np.float32)
    laid['earlier'] = np.ascontiguousarray(np.broadcast_to(
        np.tril(np.ones((EXPERTS, EXPERTS), np.float32), -1), (P, EXPERTS, EXPERTS)))

    nc = bacc.Bacc("TRN2", target_bir_lowering=False, num_devices=1)
    arrays, args = {}, []
    for name in _INS:
        arrays[f"in_{name}"] = laid[name]
        args.append(nc.dram_tensor(f"in_{name}", laid[name].shape, mybir.dt.from_np(laid[name].dtype),
                                   kind="ExternalInput").ap())
    shape = laid['L0_attn_x'].shape
    out = nc.dram_tensor("out_0", shape, F32, kind="ExternalOutput").ap()
    sandwich_kernel(nc, *args, out)
    r = run_bass_kernel_spmd(nc, [arrays], core_ids=[0])
    return r.results[0]["out_0"]
```

```python
from collections import namedtuple
from contextlib import ExitStack

import concourse.bass as bass
from concourse import mybir

ALU = mybir.AluOpType
ACT = mybir.ActivationFunctionType
AXIS_X = mybir.AxisListType.X
F32 = mybir.dt.float32
BF16 = mybir.dt.bfloat16

P = 128
DIM = 128
STATE = 64
CHUNK = 64
TOK = 512
TILES = TOK // P
CHUNKS = TOK // CHUNK
DT_RANK = 8
EXPERTS = 8
HID = 512
KT = HID // P
C_GROUP = 32
C_GROUPS = STATE // C_GROUP
PARTS = 3
GROUP = 8
GROUPS = STATE // GROUP
QUARTER = 16
QUARTERS = STATE // QUARTER
BLOCK = 16
BLOCKS = TOK // BLOCK
PAIRS = P // BLOCK
PLANES = 4
GELU_RING = 4
LN_EPS = 1e-5
RMS_EPS = 1e-6
STEPS = STATE + GROUP
FIRST = GROUP
EXPERT_AT = [4, 12, 21, 29, 37, 46, 54, 62]
UP_AT = (0, 1, 3, 4)
DOWN_AT = (5, 6, 7, 8)
ADD_AT = 8

Moments = namedtuple("Moments", "stats mean_sum mean_gap squares mean gap_part within var var_eps rstd")


def wait_for(eng, sem, count):
    if isinstance(count, int) and count <= 0:
        return
    eng.wait_ge(sem, count)


def sandwich_kernel(nc, x, norm_w, x_proj_wT, dt_proj_wT, dt_proj_b, A_log, D, out_proj_wT,
                    w_gateT, W1, b1, W2, b2, ident_in, earlier_in, out):
    B = x.shape[0]
    x_dram = x.rearrange("b (j p) d -> b p j d", p=P)
    out_dram = out.rearrange("b (j p) d -> b p j d", p=P)

    b_planes = [nc.dram_tensor(f"b_planes{i}", [PLANES, QUARTERS, BLOCK, BLOCKS * QUARTER], BF16, kind="Internal").ap()
                for i in range(2)]

    with ExitStack() as ctx:
        def sb(name, shape, dt=F32):
            return ctx.enter_context(nc.sbuf_tensor(name, shape, dt))

        def bank(name):
            return ctx.enter_context(nc.psum_tensor(name, [P, TOK], F32))

        def sem(name):
            return ctx.enter_context(nc.semaphore(name))

        ident = sb("ident", [P, P])
        ident3 = sb("ident3", [PARTS * C_GROUP, C_GROUP])
        select = sb("select", [PARTS * C_GROUP, C_GROUP], BF16)
        earlier = sb("earlier", [P, EXPERTS, EXPERTS])
        minus_half = sb("minus_half", [P, TILES])
        w_norm = sb("w_norm", [P, 1])
        w_xproj = sb("w_xproj", [P, DT_RANK + 2 * STATE])
        w_dt = sb("w_dt", [DT_RANK, DIM])
        b_dt = sb("b_dt", [P, 1])
        a_log = sb("a_log", [P, STATE])
        a_exp = sb("a_exp", [P, STATE])
        a_neg = sb("a_neg", [P, STATE])
        d_skip = sb("d_skip", [P, 1])
        w_out = sb("w_out", [P, DIM])
        w_gate = sb("w_gate", [P, EXPERTS])
        w_up = sb("w_up", [P, EXPERTS, HID])
        b_up = sb("b_up", [P, EXPERTS, KT])
        w_down = sb("w_down", [P, EXPERTS, KT, DIM])
        b_down = sb("b_down", [EXPERTS, DIM])

        x_in = [sb(f"x_in{i}", [P, TILES, DIM]) for i in range(2)]
        rms_eps = sb("rms_eps", [P, TILES])

        def moments(name):
            return Moments(*[sb(f"{name}_{part}", [P, TILES, 6] if part == "stats" else [P, TILES])
                             for part in Moments._fields])

        row_moments = moments("row")
        ffn_moments_of = moments("ffn")
        rms_t = sb("rms_t", [P, TILES])
        rms_v = sb("rms_v", [P, TILES])
        rms_e = sb("rms_e", [P, TILES])
        rms = sb("rms", [P, TILES])
        rstd_rms = sb("rstd_rms", [P, TILES])
        z_tok = sb("z_tok", [P, TILES, DIM])
        zn_tok = sb("zn_tok", [P, TILES, DIM])
        attn_ln = sb("attn_ln", [P, TILES, DIM])
        x_mid = [sb(f"x_mid{i}", [P, TILES, DIM]) for i in range(2)]
        z2_tok = zn_tok
        gate_max = sb("gate_max", [P, TILES])
        gate_l = sb("gate_l", [P, TILES, EXPERTS])
        gate_e = sb("gate_e", [P, TILES, EXPERTS])
        gate_s = sb("gate_s", [P, TILES])
        gate_r = sb("gate_r", [P, TILES])
        gate_p = sb("gate_p", [P, TILES, EXPERTS])
        above = sb("above", [P, TILES, EXPERTS, EXPERTS])
        tied = sb("tied", [P, TILES, EXPERTS, EXPERTS])
        rank = sb("rank", [P, TILES, EXPERTS])
        combine = sb("combine", [P, TILES, EXPERTS])
        ffn_acc = sb("ffn_acc", [P, TILES, DIM])
        ffn_ln = ffn_acc
        out_tile = attn_ln

        xnT = sb("xnT", [P, TOK])
        soft_pos = sb("soft_pos", [P, TOK])
        soft_abs = sb("soft_abs", [P, TOK])
        low = soft_abs[0:DT_RANK, :]
        xn_blocks = soft_pos
        combineT = soft_pos[0:EXPERTS, :]
        rest = sb("rest", [P, TOK])
        c_hi = sb("c_hi", [STATE, TOK], BF16)
        c_mid = sb("c_mid", [STATE, TOK], BF16)
        c_lo = sb("c_lo", [STATE, TOK], BF16)
        c_parts = [[sb(f"c_parts{i}_{g}", [PARTS * C_GROUP, TOK], BF16) for g in range(C_GROUPS)] for i in range(2)]
        b_part = [sb(f"b_part{s}", [P, QUARTERS, TILES, QUARTER], BF16) for s in range(PARTS)]
        u_part = [sb(f"u_part{s}", [P, TILES, DIM], BF16) for s in range(PARTS)]
        u_rows = sb("u_rows", [P, BLOCKS, DIM], BF16)
        b_spread = [sb(f"b_spread{i}", [P, BLOCK, BLOCKS, QUARTER], BF16) for i in range(2)]
        delta = [sb(f"delta{i}", [P, TOK]) for i in range(2)]
        delta_x = sb("delta_x", [P, TOK])
        decay = [sb(f"decay{i}", [P, CHUNKS * GROUP * CHUNK]) for i in range(2)]
        state = [sb(f"state{i}", [P, CHUNKS * GROUP * CHUNK]) for i in range(2)]
        term = [sb(f"term{i}", [P, TOK]) for i in range(4)]
        y_acc = [sb(f"y_acc{i}", [P, TOK]) for i in range(2)]
        z2T = sb("z2T", [P, TOK])
        hidden = [sb(f"hidden{i}", [P, TOK]) for i in range(GELU_RING)]

        drive = [bank(f"drive{i}") for i in range(2)]
        c_rows = [bank(f"c_rows{i}") for i in range(2)]
        h_bank = [bank(f"h_bank{i}") for i in range(2)]
        y_bank = bank("y_bank")
        misc = bank("misc")
        misc_tok = misc[:, :].rearrange("p (j d) -> p j d", j=TILES)
        misc_b = misc[:, 0:TILES * STATE].rearrange("p (j g n) -> p j g n", j=TILES, g=QUARTERS)
        rest_b = rest[:, 0:TILES * STATE].rearrange("p (j g n) -> p j g n", j=TILES, g=QUARTERS)
        rest_tok = rest[:, :].rearrange("p (j d) -> p j d", j=TILES)
        misc_gate = misc[:, 0:TILES * EXPERTS].rearrange("p (j e) -> p j e", j=TILES)
        y_tok = y_bank[:, :].rearrange("p (j d) -> p j d", j=TILES)

        weights_in = sem("weights_in")
        ffn_in = sem("ffn_in")
        decay_zeroed = sem("decay_zeroed")
        spread_zeroed = sem("spread_zeroed")
        half_set = sem("half_set")
        select_built = sem("select_built")
        a_exp_done = sem("a_exp_done")
        a_ready = sem("a_ready")
        x_loaded = [sem(f"x_loaded{i}") for i in range(2)]
        in_stats = sem("in_stats")
        in_halves = sem("in_halves")
        in_moments = sem("in_moments")
        in_var = sem("in_var")
        in_rstd = sem("in_rstd")
        in_rstd2 = sem("in_rstd2")
        in_rstd2v = sem("in_rstd2v")
        in_rms_e = sem("in_rms_e")
        in_rms = sem("in_rms")
        in_scales = sem("in_scales")
        z_ready = sem("z_ready")
        zn_turned = sem("zn_turned")
        xn_ready = sem("xn_ready")
        z_turned = sem("z_turned")
        skip_ready = sem("skip_ready")
        c_ready = sem("c_ready")
        c_hi_ready = sem("c_hi_ready")
        c_rest_ready = sem("c_rest_ready")
        c_mid_ready = sem("c_mid_ready")
        c_lo_ready = sem("c_lo_ready")
        c_parts_in = sem("c_parts_in")
        b_ready = sem("b_ready")
        b_hi_ready = sem("b_hi_ready")
        b_rest_ready = sem("b_rest_ready")
        b_mid_ready = sem("b_mid_ready")
        b_lo_ready = sem("b_lo_ready")
        b_stored = sem("b_stored")
        u_turned = sem("u_turned")
        u_hi_ready = sem("u_hi_ready")
        u_rest_ready = sem("u_rest_ready")
        u_mid_ready = sem("u_mid_ready")
        u_lo_ready = sem("u_lo_ready")
        u_rows_in = sem("u_rows_in")
        spread_in = [sem(f"spread_in{i}") for i in range(2)]
        low_ready = sem("low_ready")
        low_copied = sem("low_copied")
        dt_ready = sem("dt_ready")
        soft_split = sem("soft_split")
        abs_ready = sem("abs_ready")
        soft_exp_ready = sem("soft_exp_ready")
        soft_ready = sem("soft_ready")
        delta_ready = sem("delta_ready")
        drive_input_ready = sem("drive_input_ready")
        drive_shown = sem("drive_shown")
        c_shown = sem("c_shown")
        decay_ready = sem("decay_ready")
        scanned = sem("scanned")
        term_ready = sem("term_ready")
        term_added = sem("term_added")
        attn_ready = sem("attn_ready")
        attn_stats = sem("attn_stats")
        attn_halves = sem("attn_halves")
        attn_moments = sem("attn_moments")
        attn_var = sem("attn_var")
        attn_rstd = sem("attn_rstd")
        attn_normed = sem("attn_normed")
        mid_sum = sem("mid_sum")
        mid_stats = sem("mid_stats")
        mid_halves = sem("mid_halves")
        mid_moments = sem("mid_moments")
        mid_var = sem("mid_var")
        mid_rstd = sem("mid_rstd")
        z2_ready = sem("z2_ready")
        z2_turned = sem("z2_turned")
        z2T_ready = sem("z2T_ready")
        gate_shown = sem("gate_shown")
        gate_max_ready = sem("gate_max_ready")
        gate_l_ready = sem("gate_l_ready")
        gate_e_ready = sem("gate_e_ready")
        gate_s_ready = sem("gate_s_ready")
        gate_r_ready = sem("gate_r_ready")
        gate_p_ready = sem("gate_p_ready")
        compared = sem("compared")
        ties_ready = sem("ties_ready")
        ahead_ready = sem("ahead_ready")
        rank_ready = sem("rank_ready")
        combine_ready = sem("combine_ready")
        combine_turned = sem("combine_turned")
        combineT_ready = sem("combineT_ready")
        bias_shown = sem("bias_shown")
        ffn_acc_set = sem("ffn_acc_set")
        h_shown = sem("h_shown")
        hidden_ready = sem("hidden_ready")
        y_added = sem("y_added")
        expert_added = sem("expert_added")
        ffn_stats = sem("ffn_stats")
        ffn_halves = sem("ffn_halves")
        ffn_moments = sem("ffn_moments")
        ffn_var = sem("ffn_var")
        ffn_rstd = sem("ffn_rstd")
        ffn_normed = sem("ffn_normed")
        out_ready = sem("out_ready")
        out_stored = sem("out_stored")

        block = ctx.enter_context(nc.Block())

        def beats(eng, start, beat):
            start(0, 0)
            beat(0, 0, 0, ffn=False)
            with eng.Fori(1, B // 2) as i:
                beat(2 * i - 1, i - 1, 1)
                beat(2 * i, i, 0)
            beat(B - 1, B // 2 - 1, 1, more=False)
            beat(B, B // 2, 0, scan=False, more=False)

        WEIGHTS = 13
        U_LOADS = 7
        SPREAD_LOADS = BLOCK

        @block.sync
        def _(sp):
            sp.dma_start(x_in[0][:, :, :], x_dram[0]).then_inc(x_loaded[0], 16)
            sp.dma_start(ident[:, :], ident_in).then_inc(weights_in, 16)
            for s in range(PARTS):
                sp.dma_start(ident3[C_GROUP * s:C_GROUP * (s + 1), :], ident_in[0:C_GROUP, 0:C_GROUP]).then_inc(weights_in, 16)
            sp.dma_start(w_norm[:, :], norm_w.rearrange("(p a) -> p a", a=1)).then_inc(weights_in, 16)
            sp.dma_start(w_xproj[:, :], x_proj_wT).then_inc(weights_in, 16)
            sp.dma_start(w_dt[:, :], dt_proj_wT).then_inc(weights_in, 16)
            sp.dma_start(b_dt[:, :], dt_proj_b.rearrange("(p a) -> p a", a=1)).then_inc(weights_in, 16)
            sp.dma_start(a_log[:, :], A_log).then_inc(weights_in, 16)
            sp.dma_start(d_skip[:, :], D.rearrange("(p a) -> p a", a=1)).then_inc(weights_in, 16)
            sp.dma_start(w_out[:, :], out_proj_wT).then_inc(weights_in, 16)
            sp.dma_start(w_gate[:, :], w_gateT).then_inc(weights_in, 16)
            sp.dma_start(earlier[:, :, :], earlier_in).then_inc(weights_in, 16)
            sp.dma_start(x_in[1][:, :, :], x_dram[1]).then_inc(x_loaded[1], 16)

            def spread(g, par, k, only=range(BLOCK)):
                for t in only:
                    planes = b_planes[par][:, k, t, :].rearrange("(a s) x -> a s x", a=1).to_broadcast([2, PLANES, BLOCKS * QUARTER])
                    sp.dma_start(b_spread[k % 2][t:P:BLOCK, t, :, :].rearrange("s q n -> s (q n)"),
                                 planes).then_inc(spread_in[k % 2], 16)

            def c_parts_of(g, par):
                sp.wait_ge(c_lo_ready, g + 1)
                for n in range(C_GROUPS):
                    for s, part in enumerate((c_hi, c_mid, c_lo)):
                        sp.dma_start(c_parts[par][n][C_GROUP * s:C_GROUP * (s + 1), :],
                                     part[C_GROUP * n:C_GROUP * (n + 1), :]).then_inc(c_parts_in, 16)

            def b_planes_of(g, par):
                sp.wait_ge(b_lo_ready, g + 1)
                for plane, s in enumerate((0, 1, 2, 0)):
                    for k in range(QUARTERS):
                        sp.dma_start(b_planes[par][plane, k].rearrange("t (w x) -> (t w) x", w=CHUNKS),
                                     b_part[s][:, k, :, :].rearrange("p j n -> p (j n)")).then_inc(b_stored, 16)

            def u_rows_of(g):
                for pair, s in enumerate((0, 0, 0, 2, 1, 1, 1)):
                    sp.dma_start(u_rows[BLOCK * pair:BLOCK * (pair + 1), :, :].rearrange("t (w j) d -> t w (j d)", w=CHUNKS),
                                 u_part[s][:, :, :].rearrange("p j d -> p (j d)")).then_inc(u_rows_in, 16)

            c_parts_of(0, 0)
            b_planes_of(0, 0)
            sp.wait_ge(spread_zeroed, 1)
            sp.wait_ge(b_stored, 16 * PLANES * QUARTERS)
            spread(0, 0, 0)
            sp.wait_ge(u_lo_ready, 1)
            u_rows_of(0)
            spread(0, 0, 1)
            sp.dma_start(w_up[:, :, :], W1.rearrange("e p h -> p e h")).then_inc(ffn_in, 16)
            sp.dma_start(b_up[:, :, :], b1).then_inc(ffn_in, 16)
            for e in range(EXPERTS):
                sp.dma_start(w_down[:, e, :, :], W2[e].rearrange("(k p) d -> p k d", p=P)).then_inc(ffn_in, 16)
            sp.dma_start(b_down[:, :], b2).then_inc(ffn_in, 16)

            def start(b, par):
                pass

            def beat(b, half, par, ffn=True, scan=True, more=True):
                if ffn and more:
                    nxt = b + 1 if isinstance(b, int) else sp.snap(b + 1)
                    sp.wait_ge(mid_sum, b)
                    sp.dma_start(x_in[1 - par][:, :, :], x_dram[bass.ds(nxt, 1)].rearrange("a p j d -> (a p) j d")
                                 ).then_inc(x_loaded[1 - par], 16)
                for k in range(2, QUARTERS):
                    if scan:
                        sp.wait_ge(drive_shown, b * STATE + (k - 1) * QUARTER)
                        spread(b, par, k)
                    if more and k == 2:
                        c_parts_of(b + 1, 1 - par)
                if more:
                    b_planes_of(b + 1, 1 - par)
                    sp.wait_ge(b_stored, 16 * PLANES * QUARTERS * (b + 2))
                    sp.wait_ge(u_turned, b + 2)
                    spread(b + 1, 1 - par, 0)
                    sp.wait_ge(drive_shown, (b + 1) * STATE)
                    sp.wait_ge(u_lo_ready, b + 2)
                    u_rows_of(b + 1)
                    spread(b + 1, 1 - par, 1, range(BLOCK if isinstance(b, int) and b == 0 else BLOCK - 1))
                if ffn:
                    done = b - 1 if isinstance(b, int) else sp.snap(b - 1)
                    sp.wait_ge(out_ready, b)
                    sp.dma_start(out_dram[bass.ds(done, 1)].rearrange("a p j d -> (a p) j d"), out_tile[:, :, :]
                                 ).then_inc(out_stored, 16)
                    sp.wait_ge(out_stored, 16 * b)
                if more and ffn:
                    spread(b + 1, 1 - par, 1, range(BLOCK - 1, BLOCK))

            beats(sp, start, beat)

        FFN_LOADS = 3 + EXPERTS
        PREP_AT = (5, 9, 20, 22, 27, 30, 32, 36, 43, 46)

        @block.gpsimd
        def _(pool):
            nc.gpsimd.memset(rms_eps[:, :], RMS_EPS)
            nc.gpsimd.memset(minus_half[:, :], -0.5).then_inc(half_set, 1)
            pool.wait_ge(half_set, 1)

            def power(m, var_sem, rstd_sem, count):
                pool.wait_ge(var_sem, count)
                nc.gpsimd.tensor_tensor(m.rstd[:, :], m.var_eps[:, :], minus_half[:, :], ALU.pow).then_inc(rstd_sem, 1)

            def prep_rstd(g):
                m = row_moments
                power(m, in_var, in_rstd, g + 1)
                pool.wait_ge(in_rstd, g + 1)
                nc.gpsimd.tensor_tensor(rms_t[:, :], m.rstd[:, :], m.rstd[:, :], ALU.mult).then_inc(in_rstd2, 1)
                pool.wait_ge(in_rstd2, g + 1)
                nc.gpsimd.tensor_tensor(rms_v[:, :], rms_t[:, :], m.var[:, :], ALU.mult).then_inc(in_rstd2v, 1)
                pool.wait_ge(in_rstd2v, g + 1)
                nc.gpsimd.tensor_tensor(rms_e[:, :], rms_v[:, :], rms_eps[:, :], ALU.add).then_inc(in_rms_e, 1)
                pool.wait_ge(in_rms_e, g + 1)
                nc.gpsimd.tensor_tensor(rms[:, :], rms_e[:, :], minus_half[:, :], ALU.pow).then_inc(in_rms, 1)
                pool.wait_ge(in_rms, g + 1)
                nc.gpsimd.tensor_tensor(rstd_rms[:, :], rms[:, :], m.rstd[:, :], ALU.mult).then_inc(in_scales, 1)

            prep_rstd(0)

            def start(b, par):
                pass

            def beat(b, half, par, ffn=True, scan=True, more=True):
                if scan:
                    pool.wait_ge(skip_ready, b + 1)
                    for n in range(STATE):
                        done = b * STATE + n
                        pool.wait_ge(term_ready, done + 1)
                        wait_for(pool, term_added, done)
                        nc.gpsimd.tensor_tensor(y_acc[par][:, :], y_acc[par][:, :], term[n % 4][:, :],
                                                ALU.add).then_inc(term_added, 1)
                        if more and n == PREP_AT[0] + 1:
                            prep_rstd(b + 1)
                    power(row_moments, attn_var, attn_rstd, b + 1)
                    power(row_moments, mid_var, mid_rstd, b + 1)
                if ffn:
                    power(ffn_moments_of, ffn_var, ffn_rstd, b)

            beats(pool, start, beat)

        @block.scalar
        def _(act):
            act.wait_ge(weights_in, 16 * WEIGHTS)
            nc.scalar.activation(a_exp[:, :], a_log[:, :], ACT.Exp).then_inc(a_exp_done, 1)
            act.wait_ge(a_exp_done, 1)
            nc.scalar.mul(a_neg[:, :], a_exp[:, :], -1.0).then_inc(a_ready, 1)

            def prep(g, par, at):
                if at == 0:
                    act.wait_ge(zn_turned, g + 1)
                    wait_for(act, drive_input_ready, g)
                    nc.scalar.activation(xnT[:, :], misc[:, :], ACT.Copy, scale=w_norm[:, :])
                    nc.scalar.activation(xn_blocks[:, :].rearrange("p (j t w) -> p w j t", j=TILES, t=BLOCK),
                                         misc[:, :].rearrange("p (w j t) -> p w j t", w=CHUNKS, j=TILES),
                                         ACT.Copy, scale=w_norm[:, :]).then_inc(xn_ready, 1)
                if at == 1:
                    act.wait_ge(z_turned, g + 1)
                    wait_for(act, attn_ready, g - 1)
                    nc.scalar.activation(y_acc[par][:, :], misc[:, :], ACT.Copy, scale=d_skip[:, :]).then_inc(skip_ready, 1)
                if at == 2:
                    act.wait_ge(c_ready, g + 1)
                    wait_for(act, c_parts_in, 16 * PARTS * C_GROUPS * g)
                    nc.scalar.copy(c_hi[:, :], misc[0:STATE, :]).then_inc(c_hi_ready, 1)
                if at == 3:
                    act.wait_ge(c_rest_ready, g + 1)
                    nc.scalar.copy(c_mid[:, :], rest[0:STATE, :]).then_inc(c_mid_ready, 1)
                if at == 4:
                    act.wait_ge(b_ready, g + 1)
                    wait_for(act, b_stored, 16 * PLANES * QUARTERS * g)
                    nc.scalar.copy(b_part[0][:, :, :, :].rearrange("p g j n -> p j g n"), misc_b).then_inc(b_hi_ready, 1)
                if at == 5:
                    act.wait_ge(b_rest_ready, g + 1)
                    nc.scalar.copy(b_part[1][:, :, :, :].rearrange("p g j n -> p j g n"), rest_b).then_inc(b_mid_ready, 1)
                if at == 6:
                    act.wait_ge(low_ready, g + 1)
                    nc.scalar.copy(low, misc[0:DT_RANK, :]).then_inc(low_copied, 1)
                if at == 8:
                    act.wait_ge(u_turned, g + 1)
                    wait_for(act, u_rows_in, 16 * U_LOADS * g)
                    nc.scalar.copy(u_part[0][:, :, :], misc_tok).then_inc(u_hi_ready, 1)
                if at == 9:
                    act.wait_ge(u_rest_ready, g + 1)
                    nc.scalar.copy(u_part[1][:, :, :], rest_tok).then_inc(u_mid_ready, 1)
                if at == 7:
                    act.wait_ge(soft_split, g + 1)
                    nc.scalar.activation(soft_abs[:, :], misc[:, :], ACT.Abs, bias=b_dt[:, :]).then_inc(abs_ready, 1)
                    act.wait_ge(abs_ready, g + 1)
                    nc.scalar.activation(soft_abs[:, :], soft_abs[:, :], ACT.Exp, scale=-1.0).then_inc(soft_exp_ready, 1)
                    act.wait_ge(soft_exp_ready, g + 1)
                    nc.scalar.activation(soft_abs[:, :], soft_abs[:, :], ACT.Ln, bias=1.0).then_inc(soft_ready, 1)

            for at in range(10):
                prep(0, 0, at)

            def decays(r, par, g, first, last):
                for n in range(GROUP * g + first, GROUP * g + last):
                    out = decay[g % 2][:, :].rearrange("p (c n t) -> p c n t", n=GROUP, t=CHUNK)
                    nc.scalar.activation(out[:, :, n % GROUP, 1:CHUNK],
                                         delta[par][:, :].rearrange("p (c t) -> p c t", t=CHUNK)[:, :, 1:CHUNK],
                                         ACT.Exp, scale=a_neg[:, n:n + 1]).then_inc(decay_ready, 1)

            def start(b, par):
                act.wait_ge(delta_ready, b + 1)
                act.wait_ge(decay_zeroed, 1)
                decays(b, par, 0, 0, GROUP)
                decays(b, par, 1, 0, GROUP)

            prep_at = (12, 17, 19, 21, 26, 28, 29, 34, 41, 44)
            decays_at = (0, 8, 16, 24, 32, 40, 49, 57)

            def beat(b, half, par, ffn=True, scan=True, more=True):
                f = b - 1

                def gelu(e, k):
                    unit = f * EXPERTS * KT + e * KT + k
                    act.wait_ge(h_shown, unit + 1)
                    if e > 0:
                        act.wait_ge(y_added, unit + 1 - GELU_RING)
                    nc.scalar.activation(hidden[k % GELU_RING][:, :], h_bank[k % 2][:, :], ACT.Gelu,
                                         bias=b_up[:, e, k:k + 1]).then_inc(hidden_ready, 1)

                if ffn:
                    act.wait_ge(ffn_in, 16 * FFN_LOADS)
                for pos in range(STEPS):
                    for j, at in enumerate(decays_at):
                        first = 2 * (pos - at)
                        if first not in range(0, GROUP, 2):
                            continue
                        if j + 2 < GROUPS and scan:
                            g = j + 2
                            if first == 0:
                                act.wait_ge(scanned, b * STATE + GROUP * (g - 1))
                            decays(b, par, g, first, first + 2)
                        elif j + 2 >= GROUPS and more:
                            g = j + 2 - GROUPS
                            if first == 0 and g == 0:
                                act.wait_ge(delta_ready, b + 2)
                            if first == 0:
                                act.wait_ge(scanned, (b + 1) * STATE + GROUP * (g - 1))
                            decays(b + 1, 1 - par, g, first, first + 2)
                    if ffn and pos == 1:
                        act.wait_ge(z2_turned, f + 1)
                        nc.scalar.copy(z2T[:, :], misc[:, :]).then_inc(z2T_ready, 1)
                    if ffn and pos == 3:
                        act.wait_ge(gate_l_ready, f + 1)
                        nc.scalar.activation(gate_e[:, :, :], gate_l[:, :, :], ACT.Exp).then_inc(gate_e_ready, 1)
                    if more and pos in prep_at:
                        prep(b + 1, 1 - par, prep_at.index(pos))
                    if ffn and pos in EXPERT_AT:
                        for k in range(KT):
                            gelu(EXPERT_AT.index(pos), k)
                    if ffn and pos == 8:
                        act.wait_ge(combine_turned, f + 1)
                        nc.scalar.copy(combineT, misc[0:EXPERTS, :]).then_inc(combineT_ready, 1)
                    if ffn and pos == 10:
                        act.wait_ge(bias_shown, f + 1)
                        nc.scalar.copy(ffn_acc[:, :, :], misc_tok).then_inc(ffn_acc_set, 1)

            beats(act, start, beat)

        @block.tensor
        def _(pe):
            pe.wait_ge(weights_in, 16 * WEIGHTS)
            pe.wait_ge(select_built, 1)

            def block_tokens(tile, j):
                return tile[:, j * P:(j + 1) * P]

            def prep(g, at, after_post):
                if at == 0:
                    pe.wait_ge(z_ready, g + 1)
                    wait_for(pe, u_hi_ready, g)
                    wait_for(pe, u_rest_ready, g)
                    if after_post:
                        pe.wait_ge(ffn_acc_set, g - 1)
                    for j in range(TILES):
                        last = nc.tensor.transpose(misc[:, j * P:(j + 1) * P], zn_tok[:, j, :], ident[:, :])
                    last.then_inc(zn_turned, 1)
                if at == 1:
                    pe.wait_ge(xn_ready, g + 1)
                    for j in range(TILES):
                        last = nc.tensor.transpose(misc[:, j * P:(j + 1) * P], z_tok[:, j, :], ident[:, :])
                    last.then_inc(z_turned, 1)
                if at == 2:
                    pe.wait_ge(skip_ready, g + 1)
                    nc.tensor.matmul(misc[0:STATE, :], w_xproj[:, DT_RANK + STATE:], xnT[:, :],
                                     start=True, stop=True).then_inc(c_ready, 1)
                if at == 3:
                    pe.wait_ge(c_hi_ready, g + 1)
                    pe.wait_ge(c_rest_ready, g + 1)
                    for j in range(TILES):
                        last = nc.tensor.matmul(misc_b[:, j, :, :], block_tokens(xn_blocks, j), w_xproj[:, DT_RANK:DT_RANK + STATE],
                                                start=True, stop=True)
                    last.then_inc(b_ready, 1)
                if at == 4:
                    pe.wait_ge(b_hi_ready, g + 1)
                    pe.wait_ge(b_rest_ready, g + 1)
                    nc.tensor.matmul(misc[0:DT_RANK, :], w_xproj[:, 0:DT_RANK], xnT[:, :], start=True, stop=True).then_inc(low_ready, 1)
                if at == 5:
                    pe.wait_ge(low_copied, g + 1)
                    nc.tensor.matmul(misc[:, :], w_dt[:, :], low, start=True, stop=True).then_inc(dt_ready, 1)
                if at == 6:
                    pe.wait_ge(drive_input_ready, g + 1)
                    pe.wait_ge(soft_split, g + 1)
                    pe.wait_ge(abs_ready, g + 1)
                    for j in range(TILES):
                        last = nc.tensor.transpose(misc[:, j * P:(j + 1) * P], block_tokens(delta_x, j), ident[:, :])
                    last.then_inc(u_turned, 1)

            for at in range(7):
                prep(0, at, False)

            def show_drive(r, step):
                g, w = step // GROUP, step % CHUNKS
                k, first = GROUP * g // QUARTER, GROUP * g % QUARTER
                if w == 0 and first == 0:
                    pe.wait_ge(spread_in[k % 2], 16 * SPREAD_LOADS * (2 * r + k // 2 + 1))
                wait_for(pe, scanned, r * STATE + step - 1)
                bank_view = drive[step % 2][:, :].rearrange("p (n j t) -> p j n t", n=GROUP, j=TILES)
                for j in range(TILES):
                    q = TILES * w + j
                    last = nc.tensor.matmul(bank_view[:, j, :, :], u_rows[:, q, :],
                                            b_spread[k % 2][:, :, q, first:first + GROUP].rearrange("p t n -> p n t"),
                                            start=True, stop=True)
                last.then_inc(drive_shown, 1)

            def show_c(r, par, n):
                wait_for(pe, term_ready, r * STATE + n - 1)
                nc.tensor.matmul(c_rows[n % 2][:, :],
                                 select[:, n % C_GROUP:n % C_GROUP + 1].to_broadcast([PARTS * C_GROUP, P]),
                                 c_parts[par][n // C_GROUP][:, :], start=True, stop=True).then_inc(c_shown, 1)

            def states(r, par, step):
                if step == 0:
                    pe.wait_ge(c_parts_in, 16 * PARTS * C_GROUPS * (r + 1))
                    pe.wait_ge(u_rows_in, 16 * U_LOADS * (r + 1))
                if step < STATE:
                    show_drive(r, step)
                if step >= GROUP:
                    show_c(r, par, step - GROUP)

            def start(b, par):
                for step in range(FIRST):
                    states(b, par, step)

            prep_at = (13, 15, 19, 23, 29, 32, 40)

            def beat(b, half, par, ffn=True, scan=True, more=True):
                f = b - 1

                def up(e, k):
                    unit = f * EXPERTS * KT + e * KT + k
                    if e > 0 or k >= 2:
                        pe.wait_ge(hidden_ready, unit - 1)
                    nc.tensor.matmul(h_bank[k % 2][:, :], w_up[:, e, k * P:(k + 1) * P], z2T[:, :],
                                     start=True, stop=True).then_inc(h_shown, 1)

                def down(e, k):
                    unit = f * EXPERTS * KT + e * KT + k
                    pe.wait_ge(hidden_ready, unit + 1)
                    if k == 0 and e > 0:
                        pe.wait_ge(expert_added, f * EXPERTS + e)
                    for j in range(TILES):
                        last = nc.tensor.matmul(y_tok[:, j, :], hidden[k % GELU_RING][:, j * P:(j + 1) * P],
                                                w_down[:, e, k, :], start=(k == 0 and j == 0), stop=(k == KT - 1),
                                                skip_group_check=True)
                    last.then_inc(y_added, 1)

                for pos in range(STEPS):
                    if ffn and pos == 1:
                        pe.wait_ge(z2_ready, f + 1)
                        pe.wait_ge(attn_normed, f + 1)
                        for j in range(TILES):
                            last = nc.tensor.transpose(misc[:, j * P:(j + 1) * P], z2_tok[:, j, :], ident[:, :])
                        last.then_inc(z2_turned, 1)
                    if ffn and pos == 3:
                        pe.wait_ge(z2T_ready, f + 1)
                        for j in range(TILES):
                            last = nc.tensor.matmul(misc_gate[:, j, :], z2T[:, j * P:(j + 1) * P], w_gate[:, :],
                                                    start=True, stop=True)
                        last.then_inc(gate_shown, 1)
                    if ffn and pos == 8:
                        pe.wait_ge(combine_ready, f + 1)
                        pe.wait_ge(gate_l_ready, f + 1)
                        for j in range(TILES):
                            last = nc.tensor.transpose(misc[0:EXPERTS, j * P:(j + 1) * P], combine[:, j, :], ident[:, :])
                        last.then_inc(combine_turned, 1)
                    if ffn and pos == 10:
                        pe.wait_ge(combineT_ready, f + 1)
                        for j in range(TILES):
                            last = nc.tensor.matmul(misc_tok[:, j, :], combineT[:, j * P:(j + 1) * P], b_down[:, :],
                                                    start=True, stop=True)
                        last.then_inc(bias_shown, 1)
                    if scan and pos == 67:
                        pe.wait_ge(term_added, (b + 1) * STATE)
                        pe.wait_ge(u_hi_ready, b + (2 if more else 1))
                        pe.wait_ge(u_rest_ready, b + (2 if more else 1))
                        for j in range(TILES):
                            last = nc.tensor.matmul(misc_tok[:, j, :], y_acc[par][:, j * P:(j + 1) * P],
                                                    w_out[:, :], start=True, stop=True)
                        last.then_inc(attn_ready, 1)
                    if more and pos in prep_at:
                        prep(b + 1, prep_at.index(pos), ffn)
                    if ffn:
                        for e, at in enumerate(EXPERT_AT):
                            if pos - at in DOWN_AT:
                                down(e, DOWN_AT.index(pos - at))
                            if pos == at == EXPERT_AT[0]:
                                pe.wait_ge(ffn_in, 16 * FFN_LOADS)
                            if pos - at in UP_AT:
                                up(e, UP_AT.index(pos - at))
                    if scan and pos + FIRST < STEPS:
                        states(b, par, pos + FIRST)
                    if more and pos + FIRST >= STEPS:
                        states(b + 1, 1 - par, pos + FIRST - STEPS)

            beats(pe, start, beat)

        @block.vector
        def _(dve):
            for i in range(2):
                last = nc.vector.memset(decay[i][:, :], 0.0)
            last.then_inc(decay_zeroed, 1)
            for i in range(2):
                last = nc.vector.memset(b_spread[i][:, :, :, :].rearrange("p t q n -> p (t q n)").bitcast(F32), 0.0)
            last = nc.vector.memset(u_rows[96:P, :, :].rearrange("p q d -> p (q d)").bitcast(F32), 0.0)
            last.then_inc(spread_zeroed, 1)

            def token_stats(m, src, stats_sem, halves_sem, moments_sem, var_sem, count):
                for j in range(TILES):
                    last = nc.vector.bn_stats(m.stats[:, j, :], src[:, j, :])
                last.then_inc(stats_sem, 1)
                dve.wait_ge(stats_sem, count)
                nc.vector.tensor_tensor(m.mean_sum[:, :], m.stats[:, :, 1], m.stats[:, :, 4], ALU.add)
                nc.vector.tensor_tensor(m.mean_gap[:, :], m.stats[:, :, 1], m.stats[:, :, 4], ALU.subtract)
                nc.vector.tensor_tensor(m.squares[:, :], m.stats[:, :, 2], m.stats[:, :, 5], ALU.add).then_inc(halves_sem, 1)
                dve.wait_ge(halves_sem, count)
                nc.vector.tensor_scalar(m.mean[:, :], m.mean_sum[:, :], 0.5, None, ALU.mult)
                nc.vector.scalar_tensor_tensor(out=m.gap_part[:, :], in0=m.mean_gap[:, :], scalar=0.25, in1=m.mean_gap[:, :],
                                               op0=ALU.mult, op1=ALU.mult)
                nc.vector.tensor_scalar(m.within[:, :], m.squares[:, :], 1.0 / DIM, None, ALU.mult).then_inc(moments_sem, 1)
                dve.wait_ge(moments_sem, count)
                nc.vector.tensor_tensor(m.var[:, :], m.within[:, :], m.gap_part[:, :], ALU.add)
                nc.vector.scalar_tensor_tensor(out=m.var_eps[:, :], in0=m.within[:, :], scalar=LN_EPS, in1=m.gap_part[:, :],
                                               op0=ALU.add, op1=ALU.add).then_inc(var_sem, 1)

            def normalise(m, dst, src, scale):
                for j in range(TILES):
                    last = nc.vector.tensor_scalar(dst[:, j, :], src[:, j, :], m.mean[:, j:j + 1], scale[:, j:j + 1],
                                                   ALU.subtract, ALU.mult)
                return last

            def prep(g, half_g, par, at):
                if at == 0:
                    dve.wait_ge(x_loaded[par], 16 * (half_g + 1))
                    token_stats(row_moments, x_in[par], in_stats, in_halves, in_moments, in_var, g + 1)
                if at == 1:
                    dve.wait_ge(in_scales, g + 1)
                    wait_for(dve, z_turned, g)
                    normalise(row_moments, z_tok, x_in[par], row_moments.rstd)
                    normalise(row_moments, zn_tok, x_in[par], rstd_rms).then_inc(z_ready, 1)
                if at == 2:
                    dve.wait_ge(c_hi_ready, g + 1)
                    wait_for(dve, u_lo_ready, g)
                    nc.vector.tensor_tensor(rest[0:STATE, :], misc[0:STATE, :], c_hi[:, :], ALU.subtract).then_inc(c_rest_ready, 1)
                if at == 3:
                    dve.wait_ge(c_mid_ready, g + 1)
                    nc.vector.tensor_tensor(c_lo[:, :], rest[0:STATE, :], c_mid[:, :], ALU.subtract).then_inc(c_lo_ready, 1)
                if at == 4:
                    dve.wait_ge(b_hi_ready, g + 1)
                    dve.wait_ge(c_lo_ready, g + 1)
                    nc.vector.tensor_tensor(rest_b, misc_b, b_part[0][:, :, :, :].rearrange("p g j n -> p j g n"),
                                            ALU.subtract).then_inc(b_rest_ready, 1)
                if at == 5:
                    dve.wait_ge(b_mid_ready, g + 1)
                    nc.vector.tensor_tensor(b_part[2][:, :, :, :].rearrange("p g j n -> p j g n"), rest_b,
                                            b_part[1][:, :, :, :].rearrange("p g j n -> p j g n"),
                                            ALU.subtract).then_inc(b_lo_ready, 1)
                if at == 6:
                    dve.wait_ge(dt_ready, g + 1)
                    nc.vector.tensor_scalar(soft_pos[:, :], misc[:, :], b_dt[:, :], 0.0, ALU.add,
                                            ALU.max).then_inc(soft_split, 1)
                if at == 7:
                    dve.wait_ge(soft_ready, g + 1)
                    nc.vector.tensor_tensor(delta[par][:, :], soft_abs[:, :], soft_pos[:, :], ALU.add).then_inc(delta_ready, 1)
                    dve.wait_ge(delta_ready, g + 1)
                    nc.vector.tensor_tensor(delta_x[:, :].rearrange("p (j t w) -> p w j t", j=TILES, t=BLOCK),
                                            delta[par][:, :].rearrange("p (w j t) -> p w j t", w=CHUNKS, j=TILES),
                                            xnT[:, :].rearrange("p (w j t) -> p w j t", w=CHUNKS, j=TILES),
                                            ALU.mult).then_inc(drive_input_ready, 1)
                if at == 8:
                    dve.wait_ge(u_hi_ready, g + 1)
                    dve.wait_ge(b_lo_ready, g + 1)
                    nc.vector.tensor_tensor(rest_tok, misc_tok, u_part[0][:, :, :], ALU.subtract).then_inc(u_rest_ready, 1)
                if at == 9:
                    dve.wait_ge(u_mid_ready, g + 1)
                    nc.vector.tensor_tensor(u_part[2][:, :, :], rest_tok, u_part[1][:, :, :],
                                            ALU.subtract).then_inc(u_lo_ready, 1)

            prep(0, 0, 0, 0)
            dve.wait_ge(weights_in, 16 * WEIGHTS)
            nc.vector.tensor_copy(select[:, :], ident3[:, :]).then_inc(select_built, 1)
            for at in range(1, 10):
                prep(0, 0, 0, at)
            dve.wait_ge(a_ready, 1)

            def state_of(r, step):
                g, w = step // GROUP, step % CHUNKS
                if w == 0:
                    dve.wait_ge(decay_ready, r * STATE + GROUP * (g + 1))
                    wait_for(dve, term_ready, r * STATE + GROUP * (g - 1))
                dve.wait_ge(drive_shown, r * STATE + step + 1)
                part = bass.ts(w, GROUP * CHUNK)
                nc.vector.tensor_tensor_scan(state[g % 2][:, part], decay[g % 2][:, part], drive[step % 2][:, :],
                                             0.0, ALU.mult, ALU.add).then_inc(scanned, 1)

            def term_of(r, n):
                done = r * STATE + n
                g = n // GROUP
                dve.wait_ge(c_shown, done + 1)
                if n % GROUP == 0:
                    dve.wait_ge(scanned, r * STATE + GROUP * (g + 1))
                wait_for(dve, term_added, done - 3)
                states = state[g % 2][:, :].rearrange("p (c n t) -> p c n t", n=GROUP, t=CHUNK)
                nc.vector.tensor_tensor(term[n % 4][:, :].rearrange("p (c t) -> p c t", t=CHUNK),
                                        states[:, :, n % GROUP, :],
                                        c_rows[n % 2][:, :].rearrange("p (c t) -> p c t", t=CHUNK),
                                        ALU.mult).then_inc(term_ready, 1)

            def start(b, par):
                for step in range(FIRST):
                    state_of(b, step)

            def beat(b, half, par, ffn=True, scan=True, more=True):
                f = b - 1

                def close(at):
                    m = row_moments
                    if at == 0:
                        dve.wait_ge(attn_ready, b + 1)
                        token_stats(m, misc_tok, attn_stats, attn_halves, attn_moments, attn_var, b + 1)
                    if at == 1:
                        dve.wait_ge(attn_rstd, b + 1)
                        normalise(m, attn_ln, misc_tok, m.rstd).then_inc(attn_normed, 1)
                        dve.wait_ge(attn_normed, b + 1)
                        nc.vector.tensor_tensor(x_mid[par][:, :, :], attn_ln[:, :, :], x_in[par][:, :, :],
                                                ALU.add).then_inc(mid_sum, 1)
                        dve.wait_ge(mid_sum, b + 1)
                        token_stats(m, x_mid[par], mid_stats, mid_halves, mid_moments, mid_var, b + 1)
                    if at == 2:
                        dve.wait_ge(mid_rstd, b + 1)
                        normalise(m, z2_tok, x_mid[par], m.rstd).then_inc(z2_ready, 1)

                def gate(at):
                    if at == 0:
                        dve.wait_ge(gate_shown, f + 1)
                        nc.vector.tensor_reduce(gate_max[:, :], misc_gate, AXIS_X, ALU.max).then_inc(gate_max_ready, 1)
                        dve.wait_ge(gate_max_ready, f + 1)
                        nc.vector.tensor_tensor(gate_l[:, :, :], misc_gate,
                                                gate_max[:, :].rearrange("p (j a) -> p j a", a=1)
                                                .to_broadcast([P, TILES, EXPERTS]), ALU.subtract).then_inc(gate_l_ready, 1)
                    if at == 1:
                        dve.wait_ge(gate_e_ready, f + 1)
                        nc.vector.tensor_reduce(gate_s[:, :], gate_e[:, :, :], AXIS_X, ALU.add).then_inc(gate_s_ready, 1)
                        dve.wait_ge(gate_s_ready, f + 1)
                        nc.vector.reciprocal(gate_r[:, :], gate_s[:, :]).then_inc(gate_r_ready, 1)
                        dve.wait_ge(gate_r_ready, f + 1)
                        nc.vector.tensor_tensor(gate_p[:, :, :], gate_e[:, :, :],
                                                gate_r[:, :].rearrange("p (j a) -> p j a", a=1)
                                                .to_broadcast([P, TILES, EXPERTS]), ALU.mult).then_inc(gate_p_ready, 1)
                        dve.wait_ge(gate_p_ready, f + 1)
                        for j in range(TILES):
                            this = gate_p[:, j, :].rearrange("p (e a) -> p e a", a=1).to_broadcast([P, EXPERTS, EXPERTS])
                            other = gate_p[:, j, :].rearrange("p (a e) -> p a e", a=1).to_broadcast([P, EXPERTS, EXPERTS])
                            nc.vector.tensor_tensor(above[:, j, :, :], other, this, ALU.is_gt)
                            last = nc.vector.tensor_tensor(tied[:, j, :, :], other, this, ALU.is_equal)
                        last.then_inc(compared, 1)
                        dve.wait_ge(compared, f + 1)
                        nc.vector.tensor_tensor(tied[:, :, :, :].rearrange("p j e o -> p j (e o)"),
                                                tied[:, :, :, :].rearrange("p j e o -> p j (e o)"),
                                                earlier[:, :, :].rearrange("p (a e) o -> p a (e o)", a=1)
                                                .to_broadcast([P, TILES, EXPERTS * EXPERTS]),
                                                ALU.mult).then_inc(ties_ready, 1)
                        dve.wait_ge(ties_ready, f + 1)
                        nc.vector.tensor_tensor(above[:, :, :, :], above[:, :, :, :], tied[:, :, :, :],
                                                ALU.add).then_inc(ahead_ready, 1)
                        dve.wait_ge(ahead_ready, f + 1)
                        nc.vector.tensor_reduce(rank[:, :, :], above[:, :, :, :], AXIS_X, ALU.add).then_inc(rank_ready, 1)
                        dve.wait_ge(rank_ready, f + 1)
                        nc.vector.scalar_tensor_tensor(out=combine[:, :, :], in0=rank[:, :, :], scalar=1.5,
                                                       in1=gate_p[:, :, :], op0=ALU.is_lt,
                                                       op1=ALU.mult).then_inc(combine_ready, 1)

                def add_expert(e):
                    dve.wait_ge(y_added, f * EXPERTS * KT + (e + 1) * KT)
                    dve.wait_ge(ffn_acc_set, f + 1)
                    if e > 0:
                        dve.wait_ge(expert_added, f * EXPERTS + e)
                    for j in range(TILES):
                        last = nc.vector.scalar_tensor_tensor(out=ffn_acc[:, j, :], in0=y_tok[:, j, :],
                                                              scalar=combine[:, j, e:e + 1], in1=ffn_acc[:, j, :],
                                                              op0=ALU.mult, op1=ALU.add)
                    last.then_inc(expert_added, 1)

                def finish(at):
                    m = ffn_moments_of
                    if at == 0:
                        dve.wait_ge(expert_added, (f + 1) * EXPERTS)
                        token_stats(m, ffn_acc, ffn_stats, ffn_halves, ffn_moments, ffn_var, f + 1)
                    if at == 1:
                        dve.wait_ge(ffn_rstd, f + 1)
                        normalise(m, ffn_ln, ffn_acc, m.rstd).then_inc(ffn_normed, 1)
                        dve.wait_ge(ffn_normed, f + 1)
                        if not more:
                            dve.wait_ge(out_stored, 16 * f)
                        nc.vector.tensor_tensor(out_tile[:, :, :], ffn_ln[:, :, :], x_mid[1 - par][:, :, :],
                                                ALU.add).then_inc(out_ready, 1)

                for pos in range(STEPS):
                    step = pos + FIRST
                    if scan and step < STEPS:
                        if step % GROUP == 0:
                            term_of(b, step - GROUP)
                        if step < STATE:
                            state_of(b, step)
                        if step % GROUP > 0:
                            term_of(b, step - GROUP)
                    if more and step >= STEPS:
                        state_of(b + 1, step - STEPS)
                    if scan and pos in (67, 69, 71):
                        close((67, 69, 71).index(pos))
                    if ffn and pos in (2, 4):
                        gate((2, 4).index(pos))
                    if more and pos in PREP_AT:
                        prep(b + 1, half + par, 1 - par, PREP_AT.index(pos))
                    if ffn and pos - ADD_AT in EXPERT_AT:
                        add_expert(EXPERT_AT.index(pos - ADD_AT))
                    if ffn and pos in (70, 71):
                        finish((70, 71).index(pos))

            beats(dve, start, beat)


_INS = ['L0_attn_x', 'L0_attn_norm_w', 'x_proj_wT', 'dt_proj_wT', 'L0_attn_dt_proj_b', 'L0_attn_A_log', 'L0_attn_D',
        'out_proj_wT', 'w_gateT', 'L0_ffn_W1', 'b1_cols', 'L0_ffn_W2', 'L0_ffn_b2', 'ident', 'earlier']


def kernel(**inputs):
    import numpy as np
    import concourse.bacc as bacc
    from concourse.bass_utils import run_bass_kernel_spmd

    laid = {name: np.ascontiguousarray(a) for name, a in inputs.items()}
    laid['x_proj_wT'] = np.ascontiguousarray(laid['L0_attn_x_proj_w'].T)
    laid['dt_proj_wT'] = np.ascontiguousarray(laid['L0_attn_dt_proj_w'].T)
    laid['out_proj_wT'] = np.ascontiguousarray(laid['L0_attn_out_proj_w'].T)
    laid['w_gateT'] = np.ascontiguousarray(laid['L0_ffn_w_gate'].T)
    laid['b1_cols'] = np.ascontiguousarray(laid['L0_ffn_b1'].reshape(EXPERTS, KT, P).transpose(2, 0, 1))
    laid['ident'] = np.eye(P, dtype=np.float32)
    laid['earlier'] = np.ascontiguousarray(np.broadcast_to(
        np.tril(np.ones((EXPERTS, EXPERTS), np.float32), -1), (P, EXPERTS, EXPERTS)))

    nc = bacc.Bacc("TRN2", target_bir_lowering=False, num_devices=1)
    arrays, args = {}, []
    for name in _INS:
        arrays[f"in_{name}"] = laid[name]
        args.append(nc.dram_tensor(f"in_{name}", laid[name].shape, mybir.dt.from_np(laid[name].dtype),
                                   kind="ExternalInput").ap())
    shape = laid['L0_attn_x'].shape
    out = nc.dram_tensor("out_0", shape, F32, kind="ExternalOutput").ap()
    sandwich_kernel(nc, *args, out)
    r = run_bass_kernel_spmd(nc, [arrays], core_ids=[0])
    return r.results[0]["out_0"]
```

```python
from collections import namedtuple
from contextlib import ExitStack

import concourse.bass as bass
from concourse import mybir

ALU = mybir.AluOpType
ACT = mybir.ActivationFunctionType
AXIS_X = mybir.AxisListType.X
F32 = mybir.dt.float32
BF16 = mybir.dt.bfloat16

P = 128
DIM = 128
STATE = 64
CHUNK = 64
TOK = 512
TILES = TOK // P
CHUNKS = TOK // CHUNK
DT_RANK = 8
EXPERTS = 8
HID = 512
KT = HID // P
C_GROUP = 32
C_GROUPS = STATE // C_GROUP
PARTS = 3
GROUP = 8
GROUPS = STATE // GROUP
QUARTER = 16
QUARTERS = STATE // QUARTER
BLOCK = 16
BLOCKS = TOK // BLOCK
PLANES = 4
GELU_RING = 4
LN_EPS = 1e-5
RMS_EPS = 1e-6
STEPS = STATE + GROUP
FIRST = GROUP
EXPERT_AT = (6, 13, 21, 28, 39, 45, 52, 59)
UP_AT = ((5, 6, 8, 9), (12, 13, 15, 16), (21, 22, 24, 25), (28, 29, 31, 32),
         (39, 40, 41, 43), (46, 47, 49, 50), (52, 54, 56, 57), (61, 63, 64, 65))
DOWN_AT = ((10, 12, 13, 14), (17, 18, 19, 20), (26, 27, 28, 29), (33, 34, 35, 36),
           (44, 45, 47, 48), (52, 54, 55, 56), (58, 59, 60, 61), (66, 67, 68, 69))
ADD_AT = (13, 19, 28, 36, 48, 54, 61, 69)
POOL_EXPERTS = 6

Moments = namedtuple("Moments", "stats mean_sum mean_gap squares mean gap_part within var var_eps rstd")


def wait_for(eng, sem, count):
    if isinstance(count, int) and count <= 0:
        return
    eng.wait_ge(sem, count)


def sandwich_kernel(nc, x, norm_w, x_proj_wT, dt_proj_wT, dt_proj_b, A_log, D, out_proj_wT,
                    w_gateT, W1, b1, W2, b2, ident_in, earlier_in, out):
    B = x.shape[0]
    x_dram = x.rearrange("b (j p) d -> b p j d", p=P)
    out_dram = out.rearrange("b (j p) d -> b p j d", p=P)

    b_planes = [nc.dram_tensor(f"b_planes{i}", [PLANES, QUARTERS, BLOCK, BLOCKS * QUARTER], BF16, kind="Internal").ap()
                for i in range(2)]

    with ExitStack() as ctx:
        def sb(name, shape, dt=F32):
            return ctx.enter_context(nc.sbuf_tensor(name, shape, dt))

        def bank(name):
            return ctx.enter_context(nc.psum_tensor(name, [P, TOK], F32))

        def sem(name):
            return ctx.enter_context(nc.semaphore(name))

        ident = sb("ident", [P, P])
        ident3 = sb("ident3", [PARTS * C_GROUP, C_GROUP])
        select = sb("select", [PARTS * C_GROUP, C_GROUP], BF16)
        earlier = sb("earlier", [P, EXPERTS, EXPERTS])
        minus_half = sb("minus_half", [P, TILES])
        w_norm = sb("w_norm", [P, 1])
        w_xproj = sb("w_xproj", [P, DT_RANK + 2 * STATE])
        w_dt = sb("w_dt", [STATE + DT_RANK, DIM])
        b_dt = sb("b_dt", [P, 1])
        a_log = sb("a_log", [P, STATE])
        a_exp = sb("a_exp", [P, STATE])
        a_neg = sb("a_neg", [P, STATE])
        d_skip = sb("d_skip", [P, 1])
        w_out = sb("w_out", [P, DIM])
        w_gate = sb("w_gate", [P, EXPERTS])
        w_up = sb("w_up", [P, EXPERTS, HID])
        b_up = sb("b_up", [P, EXPERTS, KT])
        w_down = sb("w_down", [P, EXPERTS, KT, DIM])
        b_down = sb("b_down", [EXPERTS, DIM])

        x_in = [sb(f"x_in{i}", [P, TILES, DIM]) for i in range(2)]
        rms_eps = sb("rms_eps", [P, TILES])

        def moments(name):
            return Moments(*[sb(f"{name}_{part}", [P, TILES, 6] if part == "stats" else [P, TILES])
                             for part in Moments._fields])

        row_moments = moments("row")
        ffn_row_moments = moments("ffn")
        rms_t = sb("rms_t", [P, TILES])
        rms_v = sb("rms_v", [P, TILES])
        rms_e = sb("rms_e", [P, TILES])
        rms = sb("rms", [P, TILES])
        rstd_rms = sb("rstd_rms", [P, TILES])
        z_tok = sb("z_tok", [P, TILES, DIM])
        zn_tok = sb("zn_tok", [P, TILES, DIM])
        attn_ln = sb("attn_ln", [P, TILES, DIM])
        x_mid = [sb(f"x_mid{i}", [P, TILES, DIM]) for i in range(2)]
        z2_tok = zn_tok
        gate_max = sb("gate_max", [P, TILES])
        gate_l = sb("gate_l", [P, TILES, EXPERTS])
        gate_e = sb("gate_e", [P, TILES, EXPERTS])
        gate_s = sb("gate_s", [P, TILES])
        gate_r = sb("gate_r", [P, TILES])
        gate_p = sb("gate_p", [P, TILES, EXPERTS])
        compare = sb("compare", [P, 2, TILES, EXPERTS, EXPERTS])
        above, tied = compare[:, 0], compare[:, 1]
        weighted = compare[:, :, :, :, :].rearrange("p a j e o -> p (a j e o)").rearrange("p (j d) -> p j d", j=TILES)
        rank = sb("rank", [P, TILES, EXPERTS])
        combine = sb("combine", [P, TILES, EXPERTS])
        ffn_acc = sb("ffn_acc", [P, TILES, DIM])
        ffn_ln = ffn_acc
        out_tile = attn_ln

        xnT = sb("xnT", [P, TOK])
        soft_pos = sb("soft_pos", [P, TOK])
        soft_abs = sb("soft_abs", [P, TOK])
        low = soft_abs[STATE:STATE + DT_RANK, :]
        xn_blocks = soft_pos
        combineT = soft_pos[0:EXPERTS, :]
        rest = sb("rest", [P, TOK])
        c_hi = sb("c_hi", [STATE, TOK], BF16)
        c_mid = sb("c_mid", [STATE, TOK], BF16)
        c_lo = sb("c_lo", [STATE, TOK], BF16)
        c_parts = [[sb(f"c_parts{i}_{g}", [PARTS * C_GROUP, TOK], BF16) for g in range(C_GROUPS)] for i in range(2)]
        b_part = [sb(f"b_part{s}", [P, QUARTERS, TILES, QUARTER], BF16) for s in range(PARTS)]
        u_part = [sb(f"u_part{s}", [P, TILES, DIM], BF16) for s in range(PARTS)]
        u_rows = sb("u_rows", [P, BLOCKS, DIM], BF16)
        b_spread = [sb(f"b_spread{i}", [P, BLOCK, BLOCKS, QUARTER], BF16) for i in range(2)]
        delta = [sb(f"delta{i}", [P, TOK]) for i in range(2)]
        delta_x = sb("delta_x", [P, TOK])
        decay = [sb(f"decay{i}", [P, CHUNKS * GROUP * CHUNK]) for i in range(2)]
        state = [sb(f"state{i}", [P, CHUNKS * GROUP * CHUNK]) for i in range(2)]
        term = [sb(f"term{i}", [P, TOK]) for i in range(4)]
        y_acc = [sb(f"y_acc{i}", [P, TOK]) for i in range(2)]
        z2T = sb("z2T", [P, TOK])
        hidden = [sb(f"hidden{i}", [P, TOK]) for i in range(GELU_RING)]

        drive = [bank(f"drive{i}") for i in range(2)]
        c_rows = [bank(f"c_rows{i}") for i in range(2)]
        h_bank = [bank(f"h_bank{i}") for i in range(2)]
        y_bank = bank("y_bank")
        misc = bank("misc")
        misc_tok = misc[:, :].rearrange("p (j d) -> p j d", j=TILES)
        misc_b = misc[:, 0:TILES * STATE].rearrange("p (j g n) -> p j g n", j=TILES, g=QUARTERS)
        rest_b = rest[:, 0:TILES * STATE].rearrange("p (j g n) -> p j g n", j=TILES, g=QUARTERS)
        rest_tok = rest[:, :].rearrange("p (j d) -> p j d", j=TILES)
        misc_gate = misc[:, 0:TILES * EXPERTS].rearrange("p (j e) -> p j e", j=TILES)
        y_tok = y_bank[:, :].rearrange("p (j d) -> p j d", j=TILES)

        weights_in = sem("weights_in")
        ffn_in = sem("ffn_in")
        decay_zeroed = sem("decay_zeroed")
        spread_zeroed = sem("spread_zeroed")
        half_set = sem("half_set")
        select_built = sem("select_built")
        a_exp_done = sem("a_exp_done")
        a_ready = sem("a_ready")
        x_loaded = [sem(f"x_loaded{i}") for i in range(2)]
        in_stats = sem("in_stats")
        in_halves = sem("in_halves")
        in_moments = sem("in_moments")
        in_var = sem("in_var")
        in_rstd = sem("in_rstd")
        in_rstd_squared = sem("in_rstd_squared")
        in_rms_v = sem("in_rms_v")
        in_rms_e = sem("in_rms_e")
        in_rms = sem("in_rms")
        in_scales = sem("in_scales")
        z_ready = sem("z_ready")
        zn_turned = sem("zn_turned")
        xn_ready = sem("xn_ready")
        z_turned = sem("z_turned")
        skip_ready = sem("skip_ready")
        c_ready = sem("c_ready")
        c_hi_ready = sem("c_hi_ready")
        c_rest_ready = sem("c_rest_ready")
        c_mid_ready = sem("c_mid_ready")
        c_lo_ready = sem("c_lo_ready")
        c_parts_in = sem("c_parts_in")
        b_ready = sem("b_ready")
        b_hi_ready = sem("b_hi_ready")
        b_rest_ready = sem("b_rest_ready")
        b_mid_ready = sem("b_mid_ready")
        b_lo_ready = sem("b_lo_ready")
        b_stored = sem("b_stored")
        u_turned = sem("u_turned")
        u_hi_ready = sem("u_hi_ready")
        u_rest_ready = sem("u_rest_ready")
        u_mid_ready = sem("u_mid_ready")
        u_lo_ready = sem("u_lo_ready")
        u_rows_in = sem("u_rows_in")
        spread_in = [sem(f"spread_in{i}") for i in range(2)]
        low_copied = sem("low_copied")
        dt_ready = sem("dt_ready")
        soft_split = sem("soft_split")
        abs_ready = sem("abs_ready")
        soft_exp_ready = sem("soft_exp_ready")
        soft_ready = sem("soft_ready")
        delta_ready = sem("delta_ready")
        drive_input_ready = sem("drive_input_ready")
        drive_shown = sem("drive_shown")
        c_shown = sem("c_shown")
        decay_ready = sem("decay_ready")
        scanned = sem("scanned")
        term_ready = sem("term_ready")
        term_added = sem("term_added")
        attn_ready = sem("attn_ready")
        attn_stats = sem("attn_stats")
        attn_halves = sem("attn_halves")
        attn_moments = sem("attn_moments")
        attn_var = sem("attn_var")
        attn_rstd = sem("attn_rstd")
        attn_normed = sem("attn_normed")
        mid_sum = sem("mid_sum")
        mid_stats = sem("mid_stats")
        mid_halves = sem("mid_halves")
        mid_moments = sem("mid_moments")
        mid_var = sem("mid_var")
        mid_rstd = sem("mid_rstd")
        z2_ready = sem("z2_ready")
        z2_turned = sem("z2_turned")
        z2T_ready = sem("z2T_ready")
        gate_shown = sem("gate_shown")
        gate_max_ready = sem("gate_max_ready")
        gate_l_ready = sem("gate_l_ready")
        gate_e_ready = sem("gate_e_ready")
        gate_s_ready = sem("gate_s_ready")
        gate_r_ready = sem("gate_r_ready")
        gate_p_ready = sem("gate_p_ready")
        compared = sem("compared")
        ties_ready = sem("ties_ready")
        ahead_ready = sem("ahead_ready")
        rank_ready = sem("rank_ready")
        combine_ready = sem("combine_ready")
        combine_turned = sem("combine_turned")
        combineT_ready = sem("combineT_ready")
        bias_shown = sem("bias_shown")
        ffn_acc_set = sem("ffn_acc_set")
        h_shown = sem("h_shown")
        hidden_ready = sem("hidden_ready")
        y_added = sem("y_added")
        expert_weighted = sem("expert_weighted")
        expert_added = sem("expert_added")
        ffn_stats = sem("ffn_stats")
        ffn_halves = sem("ffn_halves")
        ffn_moments = sem("ffn_moments")
        ffn_var = sem("ffn_var")
        ffn_rstd = sem("ffn_rstd")
        ffn_normed = sem("ffn_normed")
        out_ready = sem("out_ready")
        out_stored = sem("out_stored")

        block = ctx.enter_context(nc.Block())

        def beats(eng, start, beat):
            start(0, 0)
            beat(0, 0, 0, ffn=False)
            with eng.Fori(1, B // 2) as i:
                beat(2 * i - 1, i - 1, 1)
                beat(2 * i, i, 0)
            beat(B - 1, B // 2 - 1, 1, more=False)
            beat(B, B // 2, 0, scan=False, more=False)

        WEIGHTS = 13
        U_LOADS = 7
        SPREAD_LOADS = BLOCK

        @block.sync
        def _(sp):
            sp.dma_start(x_in[0][:, :, :], x_dram[0]).then_inc(x_loaded[0], 16)
            sp.dma_start(ident[:, :], ident_in).then_inc(weights_in, 16)
            for s in range(PARTS):
                sp.dma_start(ident3[C_GROUP * s:C_GROUP * (s + 1), :], ident_in[0:C_GROUP, 0:C_GROUP]).then_inc(weights_in, 16)
            sp.dma_start(w_norm[:, :], norm_w.rearrange("(p a) -> p a", a=1)).then_inc(weights_in, 16)
            sp.dma_start(w_xproj[:, :], x_proj_wT).then_inc(weights_in, 16)
            sp.dma_start(w_dt[STATE:STATE + DT_RANK, :], dt_proj_wT).then_inc(weights_in, 16)
            sp.dma_start(b_dt[:, :], dt_proj_b.rearrange("(p a) -> p a", a=1)).then_inc(weights_in, 16)
            sp.dma_start(a_log[:, :], A_log).then_inc(weights_in, 16)
            sp.dma_start(d_skip[:, :], D.rearrange("(p a) -> p a", a=1)).then_inc(weights_in, 16)
            sp.dma_start(w_out[:, :], out_proj_wT).then_inc(weights_in, 16)
            sp.dma_start(w_gate[:, :], w_gateT).then_inc(weights_in, 16)
            sp.dma_start(earlier[:, :, :], earlier_in).then_inc(weights_in, 16)
            sp.dma_start(x_in[1][:, :, :], x_dram[1]).then_inc(x_loaded[1], 16)

            def spread(g, par, k, only=range(BLOCK)):
                for t in only:
                    planes = b_planes[par][:, k, t, :].rearrange("(a s) x -> a s x", a=1).to_broadcast([2, PLANES, BLOCKS * QUARTER])
                    sp.dma_start(b_spread[k % 2][t:P:BLOCK, t, :, :].rearrange("s q n -> s (q n)"),
                                 planes).then_inc(spread_in[k % 2], 16)

            def c_parts_of(g, par):
                sp.wait_ge(c_lo_ready, g + 1)
                for n in range(C_GROUPS):
                    for s, part in enumerate((c_hi, c_mid, c_lo)):
                        sp.dma_start(c_parts[par][n][C_GROUP * s:C_GROUP * (s + 1), :],
                                     part[C_GROUP * n:C_GROUP * (n + 1), :]).then_inc(c_parts_in, 16)

            def b_planes_of(g, par, quarters=range(QUARTERS)):
                sp.wait_ge(b_lo_ready, g + 1)
                for k in quarters:
                    for plane, s in enumerate((0, 1, 2, 0)):
                        sp.dma_start(b_planes[par][plane, k].rearrange("t (w x) -> (t w) x", w=CHUNKS),
                                     b_part[s][:, k, :, :].rearrange("p j n -> p (j n)")).then_inc(b_stored, 16)

            def u_rows_of(g):
                for pair, s in enumerate((0, 0, 0, 2, 1, 1, 1)):
                    sp.dma_start(u_rows[BLOCK * pair:BLOCK * (pair + 1), :, :].rearrange("t (w j) d -> t w (j d)", w=CHUNKS),
                                 u_part[s][:, :, :].rearrange("p j d -> p (j d)")).then_inc(u_rows_in, 16)

            b_planes_of(0, 0, range(1))
            sp.wait_ge(spread_zeroed, 2)
            sp.wait_ge(b_stored, 16 * PLANES)
            spread(0, 0, 0)
            sp.wait_ge(u_lo_ready, 1)
            u_rows_of(0)
            c_parts_of(0, 0)
            b_planes_of(0, 0, range(1, QUARTERS))
            sp.wait_ge(b_stored, 16 * PLANES * QUARTERS)
            spread(0, 0, 1)
            sp.dma_start(w_up[:, :, :], W1.rearrange("e p h -> p e h")).then_inc(ffn_in, 16)
            sp.dma_start(b_up[:, :, :], b1).then_inc(ffn_in, 16)
            for e in range(EXPERTS):
                sp.dma_start(w_down[:, e, :, :], W2[e].rearrange("(k p) d -> p k d", p=P)).then_inc(ffn_in, 16)
            sp.dma_start(b_down[:, :], b2).then_inc(ffn_in, 16)

            def start(b, par):
                pass

            def beat(b, half, par, ffn=True, scan=True, more=True):
                if ffn and more:
                    nxt = b + 1 if isinstance(b, int) else sp.snap(b + 1)
                    sp.wait_ge(mid_sum, b)
                    sp.dma_start(x_in[1 - par][:, :, :], x_dram[bass.ds(nxt, 1)].rearrange("a p j d -> (a p) j d")
                                 ).then_inc(x_loaded[1 - par], 16)
                for k in range(2, QUARTERS):
                    if scan:
                        sp.wait_ge(drive_shown, b * STATE + (k - 1) * QUARTER)
                        spread(b, par, k)
                    if more and k == 2:
                        c_parts_of(b + 1, 1 - par)
                if more:
                    b_planes_of(b + 1, 1 - par)
                    sp.wait_ge(b_stored, 16 * PLANES * QUARTERS * (b + 2))
                    sp.wait_ge(u_turned, b + 2)
                    spread(b + 1, 1 - par, 0)
                    sp.wait_ge(drive_shown, (b + 1) * STATE)
                    sp.wait_ge(u_lo_ready, b + 2)
                    u_rows_of(b + 1)
                    spread(b + 1, 1 - par, 1, range(BLOCK if isinstance(b, int) and b == 0 else BLOCK - 1))
                if ffn:
                    done = b - 1 if isinstance(b, int) else sp.snap(b - 1)
                    sp.wait_ge(out_ready, b)
                    sp.dma_start(out_dram[bass.ds(done, 1)].rearrange("a p j d -> (a p) j d"), out_tile[:, :, :]
                                 ).then_inc(out_stored, 16)
                    sp.wait_ge(out_stored, 16 * b)
                if more and ffn:
                    spread(b + 1, 1 - par, 1, range(BLOCK - 1, BLOCK))

            beats(sp, start, beat)

        FFN_LOADS = 3 + EXPERTS

        @block.gpsimd
        def _(pool):
            nc.gpsimd.memset(rms_eps[:, :], RMS_EPS)
            nc.gpsimd.memset(minus_half[:, :], -0.5).then_inc(half_set, 1)
            pool.wait_ge(half_set, 1)

            def power(m, var_sem, rstd_sem, count):
                pool.wait_ge(var_sem, count)
                nc.gpsimd.tensor_tensor(m.rstd[:, :], m.var_eps[:, :], minus_half[:, :], ALU.pow).then_inc(rstd_sem, 1)

            def prep_rstd(g):
                m = row_moments
                power(m, in_var, in_rstd, g + 1)
                pool.wait_ge(in_rstd, g + 1)
                nc.gpsimd.tensor_tensor(rms_t[:, :], m.rstd[:, :], m.rstd[:, :], ALU.mult).then_inc(in_rstd_squared, 1)
                pool.wait_ge(in_rstd_squared, g + 1)
                nc.gpsimd.tensor_tensor(rms_v[:, :], rms_t[:, :], m.var[:, :], ALU.mult).then_inc(in_rms_v, 1)
                pool.wait_ge(in_rms_v, g + 1)
                nc.gpsimd.tensor_tensor(rms_e[:, :], rms_v[:, :], rms_eps[:, :], ALU.add).then_inc(in_rms_e, 1)
                pool.wait_ge(in_rms_e, g + 1)
                nc.gpsimd.tensor_tensor(rms[:, :], rms_e[:, :], minus_half[:, :], ALU.pow).then_inc(in_rms, 1)
                pool.wait_ge(in_rms, g + 1)
                nc.gpsimd.tensor_tensor(rstd_rms[:, :], rms[:, :], m.rstd[:, :], ALU.mult).then_inc(in_scales, 1)

            def prep(g, par, at):
                if at == 0:
                    prep_rstd(g)
                if at == 1:
                    pool.wait_ge(c_mid_ready, g + 1)
                    nc.gpsimd.tensor_tensor(c_lo[:, :], rest[0:STATE, :], c_mid[:, :], ALU.subtract).then_inc(c_lo_ready, 1)
                if at == 2:
                    pool.wait_ge(b_mid_ready, g + 1)
                    nc.gpsimd.tensor_tensor(b_part[2][:, :, :, :].rearrange("p g j n -> p j g n"), rest_b,
                                            b_part[1][:, :, :, :].rearrange("p g j n -> p j g n"),
                                            ALU.subtract).then_inc(b_lo_ready, 1)
                if at == 3:
                    pool.wait_ge(soft_ready, g + 1)
                    nc.gpsimd.tensor_tensor(delta[par][:, :], soft_abs[:, :], soft_pos[:, :], ALU.add).then_inc(delta_ready, 1)
                    pool.wait_ge(delta_ready, g + 1)
                    nc.gpsimd.tensor_tensor(delta_x[:, :].rearrange("p (j t w) -> p w j t", j=TILES, t=BLOCK),
                                            delta[par][:, :].rearrange("p (w j t) -> p w j t", w=CHUNKS, j=TILES),
                                            xnT[:, :].rearrange("p (w j t) -> p w j t", w=CHUNKS, j=TILES),
                                            ALU.mult).then_inc(drive_input_ready, 1)
                if at == 4:
                    pool.wait_ge(u_mid_ready, g + 1)
                    nc.gpsimd.tensor_tensor(u_part[2][:, :, :], rest_tok, u_part[1][:, :, :],
                                            ALU.subtract).then_inc(u_lo_ready, 1)

            nc.gpsimd.memset(decay[0][:, :], 0.0)
            prep(0, 0, 0)
            nc.gpsimd.memset(b_spread[0][:, :, :, :].rearrange("p t q n -> p (t q n)").bitcast(F32), 0.0).then_inc(spread_zeroed, 1)
            nc.gpsimd.memset(decay[1][:, :], 0.0).then_inc(decay_zeroed, 1)
            for at in range(1, 5):
                prep(0, 0, at)

            prep_at = (6, 21, 31, 34, 47)

            def start(b, par):
                pass

            def beat(b, half, par, ffn=True, scan=True, more=True):
                f = b - 1
                for n in range(STATE):
                    if scan:
                        done = b * STATE + n
                        if n == 0:
                            pool.wait_ge(skip_ready, b + 1)
                        pool.wait_ge(term_ready, done + 1)
                        wait_for(pool, term_added, done)
                        nc.gpsimd.tensor_tensor(y_acc[par][:, :], y_acc[par][:, :], term[n % 4][:, :],
                                                ALU.add).then_inc(term_added, 1)
                    if more and n in prep_at:
                        prep(b + 1, 1 - par, prep_at.index(n))
                    if ffn and n in ADD_AT[:POOL_EXPERTS]:
                        e = ADD_AT.index(n)
                        pool.wait_ge(expert_weighted, f * POOL_EXPERTS + e + 1)
                        if e == 0:
                            pool.wait_ge(ffn_acc_set, f + 1)
                        else:
                            pool.wait_ge(expert_added, f * EXPERTS + e)
                        nc.gpsimd.tensor_tensor(ffn_acc[:, :, :], ffn_acc[:, :, :], weighted, ALU.add).then_inc(expert_added, 1)
                if scan:
                    power(row_moments, attn_var, attn_rstd, b + 1)
                if ffn:
                    power(ffn_row_moments, ffn_var, ffn_rstd, b)
                if scan:
                    power(row_moments, mid_var, mid_rstd, b + 1)

            beats(pool, start, beat)

        @block.scalar
        def _(act):
            act.wait_ge(weights_in, 16 * WEIGHTS)
            nc.scalar.activation(a_exp[:, :], a_log[:, :], ACT.Exp).then_inc(a_exp_done, 1)
            act.wait_ge(a_exp_done, 1)
            nc.scalar.mul(a_neg[:, :], a_exp[:, :], -1.0).then_inc(a_ready, 1)

            def prep(g, par, at):
                if at == 0:
                    act.wait_ge(zn_turned, g + 1)
                    wait_for(act, drive_input_ready, g)
                    nc.scalar.activation(xnT[:, :], misc[:, :], ACT.Copy, scale=w_norm[:, :])
                    nc.scalar.activation(xn_blocks[:, :].rearrange("p (j t w) -> p w j t", j=TILES, t=BLOCK),
                                         misc[:, :].rearrange("p (w j t) -> p w j t", w=CHUNKS, j=TILES),
                                         ACT.Copy, scale=w_norm[:, :]).then_inc(xn_ready, 1)
                if at == 1:
                    act.wait_ge(z_turned, g + 1)
                    wait_for(act, attn_ready, g - 1)
                    nc.scalar.activation(y_acc[par][:, :], misc[:, :], ACT.Copy, scale=d_skip[:, :]).then_inc(skip_ready, 1)
                if at == 2:
                    act.wait_ge(c_ready, g + 1)
                    wait_for(act, c_parts_in, 16 * PARTS * C_GROUPS * g)
                    nc.scalar.copy(c_hi[:, :], misc[0:STATE, :]).then_inc(c_hi_ready, 1)
                    nc.scalar.copy(low, misc[STATE:STATE + DT_RANK, :]).then_inc(low_copied, 1)
                if at == 3:
                    act.wait_ge(c_rest_ready, g + 1)
                    nc.scalar.copy(c_mid[:, :], rest[0:STATE, :]).then_inc(c_mid_ready, 1)
                if at == 4:
                    act.wait_ge(b_ready, g + 1)
                    wait_for(act, b_stored, 16 * PLANES * QUARTERS * g)
                    nc.scalar.copy(b_part[0][:, :, :, :].rearrange("p g j n -> p j g n"), misc_b).then_inc(b_hi_ready, 1)
                if at == 5:
                    act.wait_ge(b_rest_ready, g + 1)
                    nc.scalar.copy(b_part[1][:, :, :, :].rearrange("p g j n -> p j g n"), rest_b).then_inc(b_mid_ready, 1)
                if at == 7:
                    act.wait_ge(u_turned, g + 1)
                    wait_for(act, u_rows_in, 16 * U_LOADS * g)
                    nc.scalar.copy(u_part[0][:, :, :], misc_tok).then_inc(u_hi_ready, 1)
                if at == 8:
                    act.wait_ge(u_rest_ready, g + 1)
                    nc.scalar.copy(u_part[1][:, :, :], rest_tok).then_inc(u_mid_ready, 1)
                if at == 6:
                    act.wait_ge(soft_split, g + 1)
                    nc.scalar.activation(soft_abs[:, :], misc[:, :], ACT.Abs, bias=b_dt[:, :]).then_inc(abs_ready, 1)
                    act.wait_ge(abs_ready, g + 1)
                    nc.scalar.activation(soft_abs[:, :], soft_abs[:, :], ACT.Exp, scale=-1.0).then_inc(soft_exp_ready, 1)
                    act.wait_ge(soft_exp_ready, g + 1)
                    nc.scalar.activation(soft_abs[:, :], soft_abs[:, :], ACT.Ln, bias=1.0).then_inc(soft_ready, 1)

            for at in range(9):
                prep(0, 0, at)

            def decays(r, par, g, first, last):
                for n in range(GROUP * g + first, GROUP * g + last):
                    out = decay[g % 2][:, :].rearrange("p (c n t) -> p c n t", n=GROUP, t=CHUNK)
                    nc.scalar.activation(out[:, :, n % GROUP, 1:CHUNK],
                                         delta[par][:, :].rearrange("p (c t) -> p c t", t=CHUNK)[:, :, 1:CHUNK],
                                         ACT.Exp, scale=a_neg[:, n:n + 1]).then_inc(decay_ready, 1)

            def start(b, par):
                act.wait_ge(delta_ready, b + 1)
                act.wait_ge(decay_zeroed, 1)
                decays(b, par, 0, 0, GROUP)
                decays(b, par, 1, 0, GROUP)

            prep_at = (11, 15, 18, 19, 24, 26, 32, 43, 45)
            decays_at = (0, 9, 16, 24, 30, 40, 48, 57)

            z2T_at, gate_at, combine_at, bias_at = 2, 4, 8, 10

            def beat(b, half, par, ffn=True, scan=True, more=True):
                f = b - 1

                def gelu(e, k):
                    unit = f * EXPERTS * KT + e * KT + k
                    act.wait_ge(h_shown, unit + 1)
                    if e > 0:
                        act.wait_ge(y_added, unit + 1 - GELU_RING)
                    nc.scalar.activation(hidden[k % GELU_RING][:, :], h_bank[k % 2][:, :], ACT.Gelu,
                                         bias=b_up[:, e, k:k + 1]).then_inc(hidden_ready, 1)

                if ffn:
                    act.wait_ge(ffn_in, 16 * FFN_LOADS)
                for pos in range(STEPS):
                    if more and pos in prep_at:
                        prep(b + 1, 1 - par, prep_at.index(pos))
                    for j, at in enumerate(decays_at):
                        first = 2 * (pos - at)
                        if first not in range(0, GROUP, 2):
                            continue
                        if j + 2 < GROUPS and scan:
                            g = j + 2
                            if first == 0:
                                act.wait_ge(scanned, b * STATE + GROUP * (g - 1))
                            decays(b, par, g, first, first + 2)
                        elif j + 2 >= GROUPS and more:
                            g = j + 2 - GROUPS
                            if first == 0 and g == 0:
                                act.wait_ge(delta_ready, b + 2)
                            if first == 0:
                                act.wait_ge(scanned, (b + 1) * STATE + GROUP * (g - 1))
                            decays(b + 1, 1 - par, g, first, first + 2)
                    if ffn and pos == z2T_at:
                        act.wait_ge(z2_turned, f + 1)
                        nc.scalar.copy(z2T[:, :], misc[:, :]).then_inc(z2T_ready, 1)
                    if ffn and pos == gate_at:
                        act.wait_ge(gate_l_ready, f + 1)
                        nc.scalar.activation(gate_e[:, :, :], gate_l[:, :, :], ACT.Exp).then_inc(gate_e_ready, 1)
                    if ffn and pos in EXPERT_AT:
                        for k in range(KT):
                            gelu(EXPERT_AT.index(pos), k)
                    if ffn and pos == combine_at:
                        act.wait_ge(combine_turned, f + 1)
                        nc.scalar.copy(combineT, misc[0:EXPERTS, :]).then_inc(combineT_ready, 1)
                    if ffn and pos == bias_at:
                        act.wait_ge(bias_shown, f + 1)
                        nc.scalar.copy(ffn_acc[:, :, :], misc_tok).then_inc(ffn_acc_set, 1)

            beats(act, start, beat)

        @block.tensor
        def _(pe):
            pe.wait_ge(weights_in, 16 * WEIGHTS)

            def block_tokens(tile, j):
                return tile[:, j * P:(j + 1) * P]

            def prep(g, at, after_post):
                if at == 0:
                    pe.wait_ge(z_ready, g + 1)
                    wait_for(pe, u_hi_ready, g)
                    wait_for(pe, u_rest_ready, g)
                    if after_post:
                        pe.wait_ge(ffn_acc_set, g - 1)
                    for j in range(TILES):
                        last = nc.tensor.transpose(misc[:, j * P:(j + 1) * P], zn_tok[:, j, :], ident[:, :])
                    last.then_inc(zn_turned, 1)
                if at == 1:
                    pe.wait_ge(xn_ready, g + 1)
                    for j in range(TILES):
                        last = nc.tensor.transpose(misc[:, j * P:(j + 1) * P], z_tok[:, j, :], ident[:, :])
                    last.then_inc(z_turned, 1)
                if at == 2:
                    pe.wait_ge(skip_ready, g + 1)
                    nc.tensor.matmul(misc[0:STATE + DT_RANK, :], w_xproj[:, 0:STATE + DT_RANK], xnT[:, :],
                                     start=True, stop=True).then_inc(c_ready, 1)
                if at == 3:
                    pe.wait_ge(c_hi_ready, g + 1)
                    pe.wait_ge(low_copied, g + 1)
                    pe.wait_ge(c_rest_ready, g + 1)
                    for j in range(TILES):
                        last = nc.tensor.matmul(misc_b[:, j, :, :], block_tokens(xn_blocks, j), w_xproj[:, STATE + DT_RANK:],
                                                start=True, stop=True)
                    last.then_inc(b_ready, 1)
                if at == 4:
                    pe.wait_ge(b_hi_ready, g + 1)
                    pe.wait_ge(b_rest_ready, g + 1)
                    nc.tensor.matmul(misc[:, :], w_dt[STATE:STATE + DT_RANK, :], low, start=True, stop=True).then_inc(dt_ready, 1)
                if at == 5:
                    pe.wait_ge(drive_input_ready, g + 1)
                    pe.wait_ge(soft_split, g + 1)
                    pe.wait_ge(abs_ready, g + 1)
                    for j in range(TILES):
                        last = nc.tensor.transpose(misc[:, j * P:(j + 1) * P], block_tokens(delta_x, j), ident[:, :])
                    last.then_inc(u_turned, 1)

            for at in range(6):
                prep(0, at, False)

            def show_drive(r, step):
                g, w = step // GROUP, step % CHUNKS
                k, first = GROUP * g // QUARTER, GROUP * g % QUARTER
                if w == 0 and first == 0:
                    pe.wait_ge(spread_in[k % 2], 16 * SPREAD_LOADS * (2 * r + k // 2 + 1))
                wait_for(pe, scanned, r * STATE + step - 1)
                bank_view = drive[step % 2][:, :].rearrange("p (n j t) -> p j n t", n=GROUP, j=TILES)
                for j in range(TILES):
                    q = TILES * w + j
                    last = nc.tensor.matmul(bank_view[:, j, :, :], u_rows[:, q, :],
                                            b_spread[k % 2][:, :, q, first:first + GROUP].rearrange("p t n -> p n t"),
                                            start=True, stop=True)
                last.then_inc(drive_shown, 1)

            def show_c(r, par, n):
                wait_for(pe, term_ready, r * STATE + n - 1)
                nc.tensor.matmul(c_rows[n % 2][:, :],
                                 select[:, n % C_GROUP:n % C_GROUP + 1].to_broadcast([PARTS * C_GROUP, P]),
                                 c_parts[par][n // C_GROUP][:, :], start=True, stop=True).then_inc(c_shown, 1)

            def states(r, par, step):
                if step == 0:
                    pe.wait_ge(u_rows_in, 16 * U_LOADS * (r + 1))
                if step == GROUP:
                    if isinstance(r, int) and r == 0:
                        pe.wait_ge(select_built, 1)
                    pe.wait_ge(c_parts_in, 16 * PARTS * C_GROUPS * (r + 1))
                if step < STATE:
                    show_drive(r, step)
                if step >= GROUP:
                    show_c(r, par, step - GROUP)

            def start(b, par):
                for step in range(FIRST):
                    states(b, par, step)

            prep_at = (12, 14, 18, 23, 27, 40)

            z2T_at, gate_at, combine_at, bias_at, attn_at = 2, 4, 9, 10, 70

            def beat(b, half, par, ffn=True, scan=True, more=True):
                f = b - 1

                def up(e, k):
                    unit = f * EXPERTS * KT + e * KT + k
                    if e > 0 or k >= 2:
                        pe.wait_ge(hidden_ready, unit - 1)
                    nc.tensor.matmul(h_bank[k % 2][:, :], w_up[:, e, k * P:(k + 1) * P], z2T[:, :],
                                     start=True, stop=True).then_inc(h_shown, 1)

                def down(e, k):
                    unit = f * EXPERTS * KT + e * KT + k
                    pe.wait_ge(hidden_ready, unit + 1)
                    if k == 0 and e > POOL_EXPERTS:
                        pe.wait_ge(expert_added, f * EXPERTS + e)
                    elif k == 0 and e > 0:
                        pe.wait_ge(expert_weighted, f * POOL_EXPERTS + e)
                    for j in range(TILES):
                        last = nc.tensor.matmul(y_tok[:, j, :], hidden[k % GELU_RING][:, j * P:(j + 1) * P],
                                                w_down[:, e, k, :], start=(k == 0 and j == 0), stop=(k == KT - 1),
                                                skip_group_check=True)
                    last.then_inc(y_added, 1)

                for pos in range(STEPS):
                    if ffn and pos == z2T_at:
                        pe.wait_ge(z2_ready, f + 1)
                        pe.wait_ge(attn_normed, f + 1)
                        for j in range(TILES):
                            last = nc.tensor.transpose(misc[:, j * P:(j + 1) * P], z2_tok[:, j, :], ident[:, :])
                        last.then_inc(z2_turned, 1)
                    if ffn and pos == gate_at:
                        pe.wait_ge(z2T_ready, f + 1)
                        for j in range(TILES):
                            last = nc.tensor.matmul(misc_gate[:, j, :], z2T[:, j * P:(j + 1) * P], w_gate[:, :],
                                                    start=True, stop=True)
                        last.then_inc(gate_shown, 1)
                    if ffn and pos == combine_at:
                        pe.wait_ge(combine_ready, f + 1)
                        pe.wait_ge(gate_l_ready, f + 1)
                        for j in range(TILES):
                            last = nc.tensor.transpose(misc[0:EXPERTS, j * P:(j + 1) * P], combine[:, j, :], ident[:, :])
                        last.then_inc(combine_turned, 1)
                    if ffn and pos == bias_at:
                        pe.wait_ge(combineT_ready, f + 1)
                        for j in range(TILES):
                            last = nc.tensor.matmul(misc_tok[:, j, :], combineT[:, j * P:(j + 1) * P], b_down[:, :],
                                                    start=True, stop=True)
                        last.then_inc(bias_shown, 1)
                    if scan and pos == attn_at:
                        pe.wait_ge(term_added, (b + 1) * STATE)
                        pe.wait_ge(u_hi_ready, b + (2 if more else 1))
                        pe.wait_ge(u_rest_ready, b + (2 if more else 1))
                        for j in range(TILES):
                            last = nc.tensor.matmul(misc_tok[:, j, :], y_acc[par][:, j * P:(j + 1) * P],
                                                    w_out[:, :], start=True, stop=True)
                        last.then_inc(attn_ready, 1)
                    if more and pos in prep_at:
                        prep(b + 1, prep_at.index(pos), ffn)
                    if ffn:
                        for e in range(EXPERTS):
                            if pos in DOWN_AT[e]:
                                down(e, DOWN_AT[e].index(pos))
                            if e == 0 and pos == UP_AT[e][0]:
                                pe.wait_ge(ffn_in, 16 * FFN_LOADS)
                            if pos in UP_AT[e]:
                                up(e, UP_AT[e].index(pos))
                    if scan and pos + FIRST < STEPS:
                        states(b, par, pos + FIRST)
                    if more and pos + FIRST >= STEPS:
                        states(b + 1, 1 - par, pos + FIRST - STEPS)

            beats(pe, start, beat)

        @block.vector
        def _(dve):
            def token_stats(m, src, stats_sem, halves_sem, moments_sem, var_sem, count):
                for j in range(TILES):
                    last = nc.vector.bn_stats(m.stats[:, j, :], src[:, j, :])
                last.then_inc(stats_sem, 1)
                dve.wait_ge(stats_sem, count)
                nc.vector.tensor_tensor(m.mean_sum[:, :], m.stats[:, :, 1], m.stats[:, :, 4], ALU.add)
                nc.vector.tensor_tensor(m.mean_gap[:, :], m.stats[:, :, 1], m.stats[:, :, 4], ALU.subtract)
                nc.vector.tensor_tensor(m.squares[:, :], m.stats[:, :, 2], m.stats[:, :, 5], ALU.add).then_inc(halves_sem, 1)
                dve.wait_ge(halves_sem, count)
                nc.vector.tensor_scalar(m.mean[:, :], m.mean_sum[:, :], 0.5, None, ALU.mult)
                nc.vector.scalar_tensor_tensor(out=m.gap_part[:, :], in0=m.mean_gap[:, :], scalar=0.25, in1=m.mean_gap[:, :],
                                               op0=ALU.mult, op1=ALU.mult)
                nc.vector.tensor_scalar(m.within[:, :], m.squares[:, :], 1.0 / DIM, None, ALU.mult).then_inc(moments_sem, 1)
                dve.wait_ge(moments_sem, count)
                nc.vector.tensor_tensor(m.var[:, :], m.within[:, :], m.gap_part[:, :], ALU.add)
                nc.vector.scalar_tensor_tensor(out=m.var_eps[:, :], in0=m.within[:, :], scalar=LN_EPS, in1=m.gap_part[:, :],
                                               op0=ALU.add, op1=ALU.add).then_inc(var_sem, 1)

            def normalise(m, dst, src, scale):
                for j in range(TILES):
                    last = nc.vector.tensor_scalar(dst[:, j, :], src[:, j, :], m.mean[:, j:j + 1], scale[:, j:j + 1],
                                                   ALU.subtract, ALU.mult)
                return last

            def prep(g, half_g, par, at):
                if at == 0:
                    dve.wait_ge(x_loaded[par], 16 * (half_g + 1))
                    token_stats(row_moments, x_in[par], in_stats, in_halves, in_moments, in_var, g + 1)
                if at == 1:
                    dve.wait_ge(in_scales, g + 1)
                    wait_for(dve, z_turned, g)
                    normalise(row_moments, z_tok, x_in[par], row_moments.rstd)
                    normalise(row_moments, zn_tok, x_in[par], rstd_rms).then_inc(z_ready, 1)
                if at == 2:
                    dve.wait_ge(c_hi_ready, g + 1)
                    wait_for(dve, u_lo_ready, g)
                    nc.vector.tensor_tensor(rest[0:STATE, :], misc[0:STATE, :], c_hi[:, :], ALU.subtract).then_inc(c_rest_ready, 1)
                if at == 3:
                    dve.wait_ge(b_hi_ready, g + 1)
                    dve.wait_ge(c_lo_ready, g + 1)
                    nc.vector.tensor_tensor(rest_b, misc_b, b_part[0][:, :, :, :].rearrange("p g j n -> p j g n"),
                                            ALU.subtract).then_inc(b_rest_ready, 1)
                if at == 4:
                    dve.wait_ge(dt_ready, g + 1)
                    nc.vector.tensor_scalar(soft_pos[:, :], misc[:, :], b_dt[:, :], 0.0, ALU.add,
                                            ALU.max).then_inc(soft_split, 1)
                if at == 5:
                    dve.wait_ge(u_hi_ready, g + 1)
                    dve.wait_ge(b_lo_ready, g + 1)
                    nc.vector.tensor_tensor(rest_tok, misc_tok, u_part[0][:, :, :], ALU.subtract).then_inc(u_rest_ready, 1)

            prep(0, 0, 0, 0)
            prep(0, 0, 0, 1)
            nc.vector.memset(b_spread[1][:, :, :, :].rearrange("p t q n -> p (t q n)").bitcast(F32), 0.0)
            nc.vector.memset(u_rows[96:P, :, :].rearrange("p q d -> p (q d)").bitcast(F32), 0.0).then_inc(spread_zeroed, 1)
            prep(0, 0, 0, 2)
            prep(0, 0, 0, 3)
            dve.wait_ge(weights_in, 16 * WEIGHTS)
            nc.vector.tensor_copy(select[:, :], ident3[:, :]).then_inc(select_built, 1)
            prep(0, 0, 0, 4)
            prep(0, 0, 0, 5)
            dve.wait_ge(a_ready, 1)

            def state_of(r, step):
                g, w = step // GROUP, step % CHUNKS
                if w == 0:
                    dve.wait_ge(decay_ready, r * STATE + GROUP * (g + 1))
                    wait_for(dve, term_ready, r * STATE + GROUP * (g - 1))
                dve.wait_ge(drive_shown, r * STATE + step + 1)
                part = bass.ts(w, GROUP * CHUNK)
                nc.vector.tensor_tensor_scan(state[g % 2][:, part], decay[g % 2][:, part], drive[step % 2][:, :],
                                             0.0, ALU.mult, ALU.add).then_inc(scanned, 1)

            def term_of(r, n):
                done = r * STATE + n
                g = n // GROUP
                dve.wait_ge(c_shown, done + 1)
                if n % GROUP == 0:
                    dve.wait_ge(scanned, r * STATE + GROUP * (g + 1))
                wait_for(dve, term_added, done - 3)
                states = state[g % 2][:, :].rearrange("p (c n t) -> p c n t", n=GROUP, t=CHUNK)
                nc.vector.tensor_tensor(term[n % 4][:, :].rearrange("p (c t) -> p c t", t=CHUNK),
                                        states[:, :, n % GROUP, :],
                                        c_rows[n % 2][:, :].rearrange("p (c t) -> p c t", t=CHUNK),
                                        ALU.mult).then_inc(term_ready, 1)

            def start(b, par):
                for step in range(FIRST):
                    state_of(b, step)

            prep_at = (6, 9, 19, 25, 30, 45)

            z2_at = 0
            gate_at = (3, 4)
            finish_at = (70, 71)
            close_at = (69, 71)

            def beat(b, half, par, ffn=True, scan=True, more=True):
                f = b - 1

                def close(at):
                    m = row_moments
                    if at == 0:
                        dve.wait_ge(attn_ready, b + 1)
                        token_stats(m, misc_tok, attn_stats, attn_halves, attn_moments, attn_var, b + 1)
                    if at == 1:
                        dve.wait_ge(attn_rstd, b + 1)
                        normalise(m, attn_ln, misc_tok, m.rstd).then_inc(attn_normed, 1)
                        dve.wait_ge(attn_normed, b + 1)
                        nc.vector.tensor_tensor(x_mid[par][:, :, :], attn_ln[:, :, :], x_in[par][:, :, :],
                                                ALU.add).then_inc(mid_sum, 1)
                        dve.wait_ge(mid_sum, b + 1)
                        token_stats(m, x_mid[par], mid_stats, mid_halves, mid_moments, mid_var, b + 1)

                def enter_ffn():
                    dve.wait_ge(mid_rstd, f + 1)
                    normalise(row_moments, z2_tok, x_mid[1 - par], row_moments.rstd).then_inc(z2_ready, 1)

                def gate(at):
                    if at == 0:
                        dve.wait_ge(gate_shown, f + 1)
                        nc.vector.tensor_reduce(gate_max[:, :], misc_gate, AXIS_X, ALU.max).then_inc(gate_max_ready, 1)
                        dve.wait_ge(gate_max_ready, f + 1)
                        nc.vector.tensor_tensor(gate_l[:, :, :], misc_gate,
                                                gate_max[:, :].rearrange("p (j a) -> p j a", a=1)
                                                .to_broadcast([P, TILES, EXPERTS]), ALU.subtract).then_inc(gate_l_ready, 1)
                    if at == 1:
                        dve.wait_ge(gate_e_ready, f + 1)
                        nc.vector.tensor_reduce(gate_s[:, :], gate_e[:, :, :], AXIS_X, ALU.add).then_inc(gate_s_ready, 1)
                        dve.wait_ge(gate_s_ready, f + 1)
                        nc.vector.reciprocal(gate_r[:, :], gate_s[:, :]).then_inc(gate_r_ready, 1)
                        dve.wait_ge(gate_r_ready, f + 1)
                        nc.vector.tensor_tensor(gate_p[:, :, :], gate_e[:, :, :],
                                                gate_r[:, :].rearrange("p (j a) -> p j a", a=1)
                                                .to_broadcast([P, TILES, EXPERTS]), ALU.mult).then_inc(gate_p_ready, 1)
                        dve.wait_ge(gate_p_ready, f + 1)
                        for j in range(TILES):
                            this = gate_p[:, j, :].rearrange("p (e a) -> p e a", a=1).to_broadcast([P, EXPERTS, EXPERTS])
                            other = gate_p[:, j, :].rearrange("p (a e) -> p a e", a=1).to_broadcast([P, EXPERTS, EXPERTS])
                            nc.vector.tensor_tensor(above[:, j], other, this, ALU.is_gt)
                            last = nc.vector.tensor_tensor(tied[:, j], other, this, ALU.is_equal)
                        last.then_inc(compared, 1)
                        dve.wait_ge(compared, f + 1)
                        nc.vector.tensor_tensor(tied.rearrange("p j e o -> p j (e o)"),
                                                tied.rearrange("p j e o -> p j (e o)"),
                                                earlier[:, :, :].rearrange("p (a e) o -> p a (e o)", a=1)
                                                .to_broadcast([P, TILES, EXPERTS * EXPERTS]),
                                                ALU.mult).then_inc(ties_ready, 1)
                        dve.wait_ge(ties_ready, f + 1)
                        nc.vector.tensor_tensor(above, above, tied,
                                                ALU.add).then_inc(ahead_ready, 1)
                        dve.wait_ge(ahead_ready, f + 1)
                        nc.vector.tensor_reduce(rank[:, :, :], above, AXIS_X, ALU.add).then_inc(rank_ready, 1)
                        dve.wait_ge(rank_ready, f + 1)
                        nc.vector.scalar_tensor_tensor(out=combine[:, :, :], in0=rank[:, :, :], scalar=1.5,
                                                       in1=gate_p[:, :, :], op0=ALU.is_lt,
                                                       op1=ALU.mult).then_inc(combine_ready, 1)

                def add_expert(e):
                    dve.wait_ge(y_added, f * EXPERTS * KT + (e + 1) * KT)
                    if e > 0:
                        dve.wait_ge(expert_added, f * EXPERTS + e)
                    if e < POOL_EXPERTS:
                        nc.vector.tensor_tensor(weighted, y_tok, combine[:, :, e:e + 1].to_broadcast([P, TILES, DIM]),
                                                ALU.mult).then_inc(expert_weighted, 1)
                        return
                    for j in range(TILES):
                        last = nc.vector.scalar_tensor_tensor(out=ffn_acc[:, j, :], in0=y_tok[:, j, :],
                                                              scalar=combine[:, j, e:e + 1], in1=ffn_acc[:, j, :],
                                                              op0=ALU.mult, op1=ALU.add)
                    last.then_inc(expert_added, 1)

                def finish(at):
                    m = ffn_row_moments
                    if at == 0:
                        dve.wait_ge(expert_added, (f + 1) * EXPERTS)
                        token_stats(m, ffn_acc, ffn_stats, ffn_halves, ffn_moments, ffn_var, f + 1)
                    if at == 1:
                        dve.wait_ge(ffn_rstd, f + 1)
                        normalise(m, ffn_ln, ffn_acc, m.rstd).then_inc(ffn_normed, 1)
                        dve.wait_ge(ffn_normed, f + 1)
                        if not more:
                            dve.wait_ge(out_stored, 16 * f)
                        nc.vector.tensor_tensor(out_tile[:, :, :], ffn_ln[:, :, :], x_mid[1 - par][:, :, :],
                                                ALU.add).then_inc(out_ready, 1)

                for pos in range(STEPS):
                    step = pos + FIRST
                    if scan and step < STEPS:
                        if step % GROUP == 0:
                            term_of(b, step - GROUP)
                        if step < STATE:
                            state_of(b, step)
                        if step % GROUP > 0:
                            term_of(b, step - GROUP)
                    if more and step >= STEPS:
                        state_of(b + 1, step - STEPS)
                    if scan and pos in close_at:
                        close(close_at.index(pos))
                    if ffn and pos == z2_at:
                        enter_ffn()
                    if ffn and pos in gate_at:
                        gate(gate_at.index(pos))
                    if more and pos in prep_at:
                        prep(b + 1, half + par, 1 - par, prep_at.index(pos))
                    if ffn and pos in ADD_AT:
                        add_expert(ADD_AT.index(pos))
                    if ffn and pos in finish_at:
                        finish(finish_at.index(pos))

            beats(dve, start, beat)


_INS = ['L0_attn_x', 'L0_attn_norm_w', 'x_proj_wT', 'dt_proj_wT', 'L0_attn_dt_proj_b', 'L0_attn_A_log', 'L0_attn_D',
        'out_proj_wT', 'w_gateT', 'L0_ffn_W1', 'b1_cols', 'L0_ffn_W2', 'L0_ffn_b2', 'ident', 'earlier']


def kernel(**inputs):
    import numpy as np
    import concourse.bacc as bacc
    from concourse.bass_utils import run_bass_kernel_spmd

    laid = {name: np.ascontiguousarray(a) for name, a in inputs.items()}
    rows = laid['L0_attn_x_proj_w']
    laid['x_proj_wT'] = np.ascontiguousarray(np.concatenate(
        [rows[DT_RANK + STATE:], rows[:DT_RANK], rows[DT_RANK:DT_RANK + STATE]]).T)
    laid['dt_proj_wT'] = np.ascontiguousarray(laid['L0_attn_dt_proj_w'].T)
    laid['out_proj_wT'] = np.ascontiguousarray(laid['L0_attn_out_proj_w'].T)
    laid['w_gateT'] = np.ascontiguousarray(laid['L0_ffn_w_gate'].T)
    laid['b1_cols'] = np.ascontiguousarray(laid['L0_ffn_b1'].reshape(EXPERTS, KT, P).transpose(2, 0, 1))
    laid['ident'] = np.eye(P, dtype=np.float32)
    laid['earlier'] = np.ascontiguousarray(np.broadcast_to(
        np.tril(np.ones((EXPERTS, EXPERTS), np.float32), -1), (P, EXPERTS, EXPERTS)))

    nc = bacc.Bacc("TRN2", target_bir_lowering=False, num_devices=1)
    arrays, args = {}, []
    for name in _INS:
        arrays[f"in_{name}"] = laid[name]
        args.append(nc.dram_tensor(f"in_{name}", laid[name].shape, mybir.dt.from_np(laid[name].dtype),
                                   kind="ExternalInput").ap())
    shape = laid['L0_attn_x'].shape
    out = nc.dram_tensor("out_0", shape, F32, kind="ExternalOutput").ap()
    sandwich_kernel(nc, *args, out)
    r = run_bass_kernel_spmd(nc, [arrays], core_ids=[0])
    return r.results[0]["out_0"]
```
